# Optimizing a Trainium2 kernel written in Bass

```python
import numpy as np
import jax
import jax.numpy as jnp

def _softmax(x, axis=-1):
    return jax.nn.softmax(x, axis=axis)

def _gelu(x):
    return jax.nn.gelu(x, approximate=True)

def _silu(x):
    return jax.nn.silu(x)

def _sigmoid(x):
    return jax.nn.sigmoid(x)

def _layernorm(x, axis=-1, eps=1e-05):
    m = jnp.mean(x, axis=axis, keepdims=True)
    v = jnp.var(x, axis=axis, keepdims=True)
    return (x - m) / jnp.sqrt(v + eps)

def _scatter_add(tgt, idx, src, axis=0):
    return tgt.at[idx].add(src)

def _segment_sum(src, seg, n):
    return jax.ops.segment_sum(src, seg, n)
kernel_name = 'mk_adaln_d1_jaxref_r4_f7cf9a'

def setup_inputs(seed: int=0):
    np.random.seed(seed)
    _w = jnp.asarray

    def _L0_attn_setup():
        import jax, jax.numpy as jnp
        import numpy as np
        DIM = 512
        B, T = (8, 512)

        def _layernorm(x, g, b, eps=1e-05):
            m = jnp.mean(x, axis=-1, keepdims=True)
            v = jnp.mean(jnp.square(x - m), axis=-1, keepdims=True)
            return (x - m) / jnp.sqrt(v + eps) * g + b

        def _shift(x):
            return jnp.pad(x[:, :-1, :], ((0, 0), (1, 0), (0, 0)))
        key = jax.random.key(seed)
        ks = jax.random.split(key, 16)
        d = DIM
        s = 0.02
        inp = {'x': jax.random.normal(ks[0], (B, T, d), dtype=jnp.float32), 'ln1_g': jnp.ones((d,), jnp.float32), 'ln1_b': jnp.zeros((d,), jnp.float32), 'ln2_g': jnp.ones((d,), jnp.float32), 'ln2_b': jnp.zeros((d,), jnp.float32), 'tm_w': jnp.zeros((d,), jnp.float32), 'tm_u': jnp.zeros((d,), jnp.float32), 'tm_mu_r': jax.random.uniform(ks[1], (d,), jnp.float32), 'tm_mu_k': jax.random.uniform(ks[2], (d,), jnp.float32), 'tm_mu_v': jax.random.uniform(ks[3], (d,), jnp.float32), 'tm_Wr': jax.random.normal(ks[4], (d, d), jnp.float32) * s, 'tm_Wk': jax.random.normal(ks[5], (d, d), jnp.float32) * s, 'tm_Wv': jax.random.normal(ks[6], (d, d), jnp.float32) * s, 'tm_Wout': jax.random.normal(ks[7], (d, d), jnp.float32) * s, 'cm_mu_r': jax.random.uniform(ks[8], (d,), jnp.float32), 'cm_mu_k': jax.random.uniform(ks[9], (d,), jnp.float32), 'cm_Wr': jax.random.normal(ks[10], (d, d), jnp.float32) * s, 'cm_Wk': jax.random.normal(ks[11], (d, d), jnp.float32) * s, 'cm_Wv': jax.random.normal(ks[12], (d, d), jnp.float32) * s}
        return inp
    _L0_attn_in = _L0_attn_setup()

    def _L0_ffn_setup():
        import jax, jax.numpy as jnp
        import numpy as np
        D = 512
        F = 352
        E = 8
        K = 2
        FS = 704
        B, S = (2, 256)
        key = jax.random.key(seed)
        ks = jax.random.split(key, 9)
        sc = 0.02
        return {'x': jax.random.normal(ks[0], (B, S, D), dtype=jnp.float32), 'Wr': jax.random.normal(ks[1], (E, D), dtype=jnp.float32) * sc, 'Wg': jax.random.normal(ks[2], (E, F, D), dtype=jnp.float32) * sc, 'Wu': jax.random.normal(ks[3], (E, F, D), dtype=jnp.float32) * sc, 'Wd': jax.random.normal(ks[4], (E, D, F), dtype=jnp.float32) * sc, 'Wsg': jax.random.normal(ks[5], (FS, D), dtype=jnp.float32) * sc, 'Wsu': jax.random.normal(ks[6], (FS, D), dtype=jnp.float32) * sc, 'Wsd': jax.random.normal(ks[7], (D, FS), dtype=jnp.float32) * sc}
    _L0_ffn_in = _L0_ffn_setup()
    _L0_c = _w((lambda *s: np.random.randn(*s).astype(np.float32) * 0.05)(4, 512))
    _L0_wmod = _w((lambda *s: np.random.randn(*s).astype(np.float32) * 0.05)(512, 6 * 512) * 512 ** (-0.5))
    _d = {'L0_attn_x': _L0_attn_in['x'], 'L0_attn_ln1_g': _L0_attn_in['ln1_g'], 'L0_attn_ln1_b': _L0_attn_in['ln1_b'], 'L0_attn_ln2_g': _L0_attn_in['ln2_g'], 'L0_attn_ln2_b': _L0_attn_in['ln2_b'], 'L0_attn_tm_w': _L0_attn_in['tm_w'], 'L0_attn_tm_u': _L0_attn_in['tm_u'], 'L0_attn_tm_mu_r': _L0_attn_in['tm_mu_r'], 'L0_attn_tm_mu_k': _L0_attn_in['tm_mu_k'], 'L0_attn_tm_mu_v': _L0_attn_in['tm_mu_v'], 'L0_attn_tm_Wr': _L0_attn_in['tm_Wr'], 'L0_attn_tm_Wk': _L0_attn_in['tm_Wk'], 'L0_attn_tm_Wv': _L0_attn_in['tm_Wv'], 'L0_attn_tm_Wout': _L0_attn_in['tm_Wout'], 'L0_attn_cm_mu_r': _L0_attn_in['cm_mu_r'], 'L0_attn_cm_mu_k': _L0_attn_in['cm_mu_k'], 'L0_attn_cm_Wr': _L0_attn_in['cm_Wr'], 'L0_attn_cm_Wk': _L0_attn_in['cm_Wk'], 'L0_attn_cm_Wv': _L0_attn_in['cm_Wv'], 'L0_ffn_Wr': _L0_ffn_in['Wr'], 'L0_ffn_Wg': _L0_ffn_in['Wg'], 'L0_ffn_Wu': _L0_ffn_in['Wu'], 'L0_ffn_Wd': _L0_ffn_in['Wd'], 'L0_ffn_Wsg': _L0_ffn_in['Wsg'], 'L0_ffn_Wsu': _L0_ffn_in['Wsu'], 'L0_ffn_Wsd': _L0_ffn_in['Wsd'], 'L0_c': _L0_c, 'L0_wmod': _L0_wmod}
    _x0 = _d['L0_attn_x']
    _d['L0_attn_x'] = jax.random.normal(jax.random.fold_in(jax.random.key(seed), 1), (4, 1024, 512), dtype=_x0.dtype)
    del _x0
    return _d

def reference(L0_attn_x, L0_attn_ln1_g, L0_attn_ln1_b, L0_attn_ln2_g, L0_attn_ln2_b, L0_attn_tm_w, L0_attn_tm_u, L0_attn_tm_mu_r, L0_attn_tm_mu_k, L0_attn_tm_mu_v, L0_attn_tm_Wr, L0_attn_tm_Wk, L0_attn_tm_Wv, L0_attn_tm_Wout, L0_attn_cm_mu_r, L0_attn_cm_mu_k, L0_attn_cm_Wr, L0_attn_cm_Wk, L0_attn_cm_Wv, L0_ffn_Wr, L0_ffn_Wg, L0_ffn_Wu, L0_ffn_Wd, L0_ffn_Wsg, L0_ffn_Wsu, L0_ffn_Wsd, L0_c, L0_wmod):

    def _L0_attn_ref(x, ln1_g, ln1_b, ln2_g, ln2_b, tm_w, tm_u, tm_mu_r, tm_mu_k, tm_mu_v, tm_Wr, tm_Wk, tm_Wv, tm_Wout, cm_mu_r, cm_mu_k, cm_Wr, cm_Wk, cm_Wv):
        import jax, jax.numpy as jnp
        import numpy as np
        DIM = 512
        B, T = (8, 512)

        def _layernorm(x, g, b, eps=1e-05):
            m = jnp.mean(x, axis=-1, keepdims=True)
            v = jnp.mean(jnp.square(x - m), axis=-1, keepdims=True)
            return (x - m) / jnp.sqrt(v + eps) * g + b

        def _shift(x):
            return jnp.pad(x[:, :-1, :], ((0, 0), (1, 0), (0, 0)))
        h = _layernorm(x, ln1_g, ln1_b)
        hp = _shift(h)
        xr = tm_mu_r * h + (1.0 - tm_mu_r) * hp
        xk = tm_mu_k * h + (1.0 - tm_mu_k) * hp
        xv = tm_mu_v * h + (1.0 - tm_mu_v) * hp
        r = jax.nn.sigmoid(jnp.einsum('btc,dc->btd', xr, tm_Wr))
        k = jnp.einsum('btc,dc->btd', xk, tm_Wk)
        v = jnp.einsum('btc,dc->btd', xv, tm_Wv)
        ek = jnp.exp(tm_u + k)
        wkv = ek * v / (ek + 1e-08)
        x = x + jnp.einsum('btc,dc->btd', r * wkv, tm_Wout)
        h2 = _layernorm(x, ln2_g, ln2_b)
        h2p = _shift(h2)
        xr2 = cm_mu_r * h2 + (1.0 - cm_mu_r) * h2p
        xk2 = cm_mu_k * h2 + (1.0 - cm_mu_k) * h2p
        r2 = jax.nn.sigmoid(jnp.einsum('btc,dc->btd', xr2, cm_Wr))
        k2 = jnp.square(jax.nn.relu(jnp.einsum('btc,dc->btd', xk2, cm_Wk)))
        x = x + r2 * jnp.einsum('btc,dc->btd', k2, cm_Wv)
        return x

    def _L0_ffn_ref(x, Wr, Wg, Wu, Wd, Wsg, Wsu, Wsd):
        import jax, jax.numpy as jnp
        import numpy as np
        D = 512
        F = 352
        E = 8
        K = 2
        FS = 704
        B, S = (2, 256)
        silu = jax.nn.silu
        sg = silu(jnp.einsum('bsd,fd->bsf', x, Wsg))
        su = jnp.einsum('bsd,fd->bsf', x, Wsu)
        shared_out = jnp.einsum('bsf,df->bsd', sg * su, Wsd)
        logits = jnp.einsum('bsd,ed->bse', x, Wr)
        scores = jax.nn.softmax(logits, axis=-1)
        topk_scores, topk_idx = jax.lax.top_k(scores, K)
        w_full = jnp.sum(jax.nn.one_hot(topk_idx, E, dtype=x.dtype) * topk_scores[..., None], axis=-2)
        g = silu(jnp.einsum('bsd,efd->bsef', x, Wg))
        u = jnp.einsum('bsd,efd->bsef', x, Wu)
        out_e = jnp.einsum('bsef,edf->bsed', g * u, Wd)
        routed_out = jnp.einsum('bsed,bse->bsd', out_e, w_full)
        return routed_out + shared_out
    x = L0_attn_x
    mod = (_silu(L0_c) @ L0_wmod).reshape(L0_c.shape[0], 6, 1, -1)
    sa, ca, ga, sb, cb, gb = (mod[:, 0], mod[:, 1], mod[:, 2], mod[:, 3], mod[:, 4], mod[:, 5])
    ga = (2 * (ga >= 0) - 1) * jnp.maximum(jnp.abs(ga), 0.25)
    gb = (2 * (gb >= 0) - 1) * jnp.maximum(jnp.abs(gb), 0.25)
    h = _layernorm(x, axis=-1) * (1 + ca) + sa
    x = x + ga * _L0_attn_ref(h, L0_attn_ln1_g, L0_attn_ln1_b, L0_attn_ln2_g, L0_attn_ln2_b, L0_attn_tm_w, L0_attn_tm_u, L0_attn_tm_mu_r, L0_attn_tm_mu_k, L0_attn_tm_mu_v, L0_attn_tm_Wr, L0_attn_tm_Wk, L0_attn_tm_Wv, L0_attn_tm_Wout, L0_attn_cm_mu_r, L0_attn_cm_mu_k, L0_attn_cm_Wr, L0_attn_cm_Wk, L0_attn_cm_Wv)
    h = _layernorm(x, axis=-1) * (1 + cb) + sb
    x = x + gb * _L0_ffn_ref(h, L0_ffn_Wr, L0_ffn_Wg, L0_ffn_Wu, L0_ffn_Wd, L0_ffn_Wsg, L0_ffn_Wsu, L0_ffn_Wsd)
    return x

_drawn_inputs = setup_inputs


def setup_inputs(seed=0):
    import zlib

    import numpy as np

    out = dict(_drawn_inputs(seed))
    spreads = {'L0_attn_ln1_g': (1.0, 0.2),
     'L0_attn_ln1_b': (0.0, 0.1),
     'L0_attn_ln2_g': (1.0, 0.2),
     'L0_attn_ln2_b': (0.0, 0.1),
     'L0_attn_tm_w': (0.0, 0.1),
     'L0_attn_tm_u': (0.0, 0.1)}
    factors = {}
    for name, (base, spread) in spreads.items():
        noise = np.random.default_rng([zlib.crc32(name.encode()), seed]).standard_normal(out[name].shape)
        drawn = base * np.exp(spread * noise) if base else spread * noise
        out[name] = jnp.asarray(drawn.astype(out[name].dtype))
    for name, factor in factors.items():
        out[name] = (out[name] * factor).astype(out[name].dtype)
    return out
```

```python
from contextlib import ExitStack

import concourse.bass as bass
from concourse import mybir

ALU = mybir.AluOpType
ACT = mybir.ActivationFunctionType
AX = mybir.AxisListType
F32 = mybir.dt.float32
F32R = mybir.dt.float32r
I32 = mybir.dt.int32

P = 128
D = 512
C = D // P
B, T = 4, 1024
N = B * T
NT = N // P
TPB = T // P
EPS = 1e-5
E = 8
F = 352
FK = -(-F // P)
GU = 2 * F
RAW = C * GU + FK * D
R = 2 * P
NJ = (2 * N + E * (R - 1)) // R
ZERO_ROWS = NJ * R // NT
ZERO_REPEAT = 3
assert ZERO_ROWS * NT == NJ * R and ZERO_ROWS % ZERO_REPEAT == 0
LN_1E8 = 18.420680743952367


class Steps:

    def __init__(self, sem, *names):
        self.sem = sem
        self.at = {name: i + 1 for i, name in enumerate(names)}

    def done(self, n, name):
        return self.sem, n * len(self.at) + self.at[name]


class Apart:

    def __init__(self, sem, prefix, *names):
        self.sem_of = {name: sem(f"{prefix}_{name}") for name in names}

    def done(self, n, name):
        return self.sem_of[name], n + 1


class Tile:

    def __init__(self, pair, offset, count):
        self.pair, self.offset, self.count = pair, offset, count
        self.p = offset % 2
        self.n = offset if pair is None else 2 * pair + offset
        self.half = offset // 2 if pair is None else pair + offset // 2

    def back(self, d):
        return Tile(self.pair, self.offset - d, self.count)

    def unit(self, half):
        return Unit(2 * self.n + half, half)

    def real(self):
        return self.pair is not None or 0 <= self.offset < self.count


class Unit:
    def __init__(self, n, half):
        self.n, self.half = n, half

    def back(self, d):
        return Unit(self.n - d, (self.half - d) % 2)


def sweep(eng, count, lead, lag, body):
    low = lag + 2 + lag % 2
    high = count - lead - (count - lead) % 2
    for t in range(-lead, low):
        body(Tile(None, t, count))
    with eng.Fori(0, (high - low) // 2) as k:
        for j in range(2):
            body(Tile(k, low + j, count))
    for t in range(high, count + lag):
        body(Tile(None, t, count))


def in_turn(*stages):
    def body(t):
        for stage_of, lag in stages:
            s = t.back(lag)
            if s.real():
                stage_of(s)
    lags = [lag for _, lag in stages]
    return max(0, -min(lags)), max(0, max(lags)), body


def build(nc, io, out):
    x_d = io["x"].rearrange("b t d -> (b t) d")
    out_d = out.rearrange("b t d -> (b t) d")

    def scratch(name, shape, dt=F32):
        return nc.dram_tensor(name, shape, dt).ap()

    mod_d = scratch("mod_rows", [B, 6 * D])
    h_d = scratch("h_rows", [N, D])
    o_d = scratch("timemix_rows", [N, D])
    x2_d = scratch("x2_rows", [N, D])
    xres_d = scratch("xres_rows", [N, D])
    h3_d = scratch("h3_rows", [N, D])
    base_d = scratch("base_rows", [N, D])
    xs_d = scratch("expert_in_rows", [NJ * R, D])
    ys_d = scratch("expert_out_rows", [NJ * R, D])

    ctx = ExitStack()
    with ctx:
        def sb(name, shape, dt=F32, at=ctx):
            return at.enter_context(nc.sbuf_tensor(name, shape, dt))

        def sem(name):
            return ctx.enter_context(nc.semaphore(name))

        def pair_of_sems(name):
            return [sem(f"{name}{p}") for p in range(2)]

        def steps(name, *names):
            return Steps(sem(name), *names)

        def flat(ap):
            return ap.rearrange("p a b -> p (a b)")

        psum = [ctx.enter_context(nc.psum_tensor(f"bank{i}", [P, D], F32)) for i in range(8)]

        ident = sb("ident", [P, P])
        keep = sb("keep", [P, NT * C])
        keep_i = sb("keep_i", [P, NT * C], I32)
        eps = sb("eps", [P, 1])
        minus_half = sb("minus_half", [P, 1])
        vecs = sb("vecs", [P, 9, C])
        G1, B1, G2, B2, MUR, MUK, MUV, MUR2, MUK2 = range(9)

        logits = sb("logits", [P, NT, 8])
        wrt = sb("wrt", [P, C, 8])
        wrt_hl = sb("wrt_hl", [P, C, 16], F32R)
        wrt_hi, wrt_lo = wrt_hl[:, :, 0:8], wrt_hl[:, :, 8:16]
        bridge_col = sb("bridge_col", [P, 4])
        zero_rows = sb("zero_rows", [P, D])

        W1 = ["r", "k", "v", "o"]
        W2 = ["r2", "k2", "v2"]
        hi, lo = {}, {}
        mixing = ctx.enter_context(ExitStack())
        with ExitStack() as time_mix:
            for w in W1:
                hi[w], lo[w] = sb(f"w_{w}_hi", [P, C, D], F32R, time_mix), sb(f"w_{w}_lo", [P, C, D], F32R, time_mix)

        hin_t = sb("hin_t", [P, 2, D], at=mixing)
        oin_t = sb("oin_t", [P, 2, D], at=mixing)
        x2_t = sb("x2_t", [P, 2, D], at=mixing)
        xh2 = sb("xh2", [P, 2, D], at=mixing)
        diff2 = sb("diff2", [P, C, P], at=mixing)
        mix2 = sb("mix2", [P, 2, C, P], at=mixing)
        xm2_hi = sb("xm2_hi", [P, 2, 2, C, P], F32R, mixing)
        xm2_lo = sb("xm2_lo", [P, 2, 2, C, P], F32R, mixing)
        k2_t = sb("k2_t", [P, D], at=mixing)
        k2_hi = sb("k2_hi", [P, C, P], F32R, mixing)
        k2_lo = sb("k2_lo", [P, C, P], F32R, mixing)
        y_t = sb("y_t", [P, D], at=mixing)
        x2r_t = sb("x2r_t", [P, 2, D], at=mixing)
        xr_t = sb("xr_t", [P, 2, D], at=mixing)
        h3_t = sb("h3_t", [P, 2, D], at=mixing)
        sr2 = sb("sr2", [P, 2, D], at=mixing)
        h3_hi = sb("h3_hi", [P, C, P], F32R, mixing)
        with ExitStack() as first:
            wmod = sb("wmod", [P, C, 6 * D], at=first)
        region2 = mixing.enter_context(ExitStack())
        for w in W2:
            hi[w], lo[w] = sb(f"w_{w}_hi", [P, C, D], F32R, region2), sb(f"w_{w}_lo", [P, C, D], F32R, region2)

        with ExitStack() as a1:
            mod1 = sb("mod1", [P, B, 2, D], at=a1)
            x_t = sb("x_t", [P, 2, D], at=a1)
            st1 = sb("st1", [P, 2, 6], at=a1)
            mv1 = sb("mv1", [P, 2, 2], at=a1)
            rstd1 = sb("rstd1", [P, 2, 1], at=a1)
            st1h = sb("st1h", [P, 2, 6], at=a1)
            mv1h = sb("mv1h", [P, 2, 2], at=a1)
            rstd1h = sb("rstd1h", [P, 2, 1], at=a1)
            var1 = sb("var1", [P, 2], at=a1)
            xh = sb("xh", [P, D], at=a1)
            h_t = sb("h_t", [P, 2, D], at=a1)
            hh = sb("hh", [P, 2, D], at=a1)
            h1T = sb("h1T", [P, 2, C, P + 1], at=a1)
            diff1 = sb("diff1", [P, C, P], at=a1)
            stage = [sb(f"stage{i}", [P, C * D], at=a1) for i in range(2)]
            mix1 = stage[0][:, 0:3 * D].rearrange("p (m c t) -> p m c t", m=3, c=C)
            z_t = stage[1][:, 0:D]
            sk_t = stage[1][:, D:2 * D]
            vk_t = stage[1][:, 2 * D:3 * D]
            rw_t = stage[1][:, 3 * D:4 * D]
            sr_more = sb("sr_more", [P, D], at=a1)
            sr_t = [stage[0][:, 3 * D:4 * D], sr_more[:]]
            xm_hi = sb("xm_hi", [P, 2, 3, C, P], F32R, a1)
            xm_lo = sb("xm_lo", [P, 2, 3, C, P], F32R, a1)
            u_bc = sb("u_bc", [P, D], at=a1)
            rw_hi = sb("rw_hi", [P, C, P], F32R, a1)
            rw_lo = sb("rw_lo", [P, C, P], F32R, a1)
            o_t = sb("o_t", [P, 2, D], at=a1)
            cT = sb("cT", [P, C, B], at=a1)
            mod_rows = [ring[0:B, p, :] for ring in (h_t, hh, o_t) for p in range(2)]
            gate_sign, gate_neg = xh[0:B, :], flat(diff1[0:B, :, :])

        with ExitStack() as a2:
            mod2 = sb("mod2", [P, B, 3, D], at=a2)
            st2 = sb("st2", [P, 2, 6], at=a2)
            mv2 = sb("mv2", [P, 2, 2], at=a2)
            var2 = sb("var2", [P, 2], at=a2)
            rstd2 = sb("rstd2", [P, 2, 1], at=a2)
            st3 = sb("st3", [P, 2, 6], at=a2)
            mv3 = sb("mv3", [P, 2, 2], at=a2)
            rstd3 = sb("rstd3", [P, 2, 1], at=a2)
            lg_part = sb("lg_part", [P, 2, 8], at=a2)
            pool_col = sb("pool_col", [P, 1], at=a2)
            h2T = sb("h2T", [P, 2, C, P + 1], at=a2)
            h3_lo = sb("h3_lo", [P, C, P], F32R, a2)

        mixing.close()

        gu_hi, gu_lo, dn_hi, dn_lo = [], [], [], []

        def expert_weights(i, at):
            gu_hi.append(sb(f"gu{i}_hi", [P, C, GU], F32R, at))
            gu_lo.append(sb(f"gu{i}_lo", [P, C, GU], F32R, at))
            dn_hi.append(sb(f"dn{i}_hi", [P, FK, D], F32R, at))
            dn_lo.append(sb(f"dn{i}_lo", [P, FK, D], F32R, at))

        raw = [sb(f"raw{i}", [P, RAW]) for i in range(2)]
        ex_x = sb("ex_x", [P, 2, D])
        ex_x_hi = sb("ex_x_hi", [P, 2, C, P], F32R)
        ex_x_lo = sb("ex_x_lo", [P, 2, C, P], F32R)
        sg_t = sb("sg_t", [P, F])
        hid = sb("hid", [P, 2, FK * P])
        hid_hi = sb("hid_hi", [P, FK, P], F32R)
        hid_lo = sb("hid_lo", [P, FK, P], F32R)
        y_rows = sb("y_rows", [P, 2, D])
        sc_t = [y_rows[:, i, :] for i in range(2)]
        w1 = sb("w1", [P, NT, 1])
        w2 = sb("w2", [P, NT, 1])
        slots = sb("slots", [P, 2, NT], I32)
        eid = sb("eid", [P, NJ], I32)
        expert_weights(2, ctx)
        with ExitStack() as before_experts:
            at = before_experts
            mod3 = sb("mod3", [P, B, D], at=at)
            base_t = sb("base_t", [P, 2, D], at=at)
            xres_t = sb("xres_t", [P, 2, D], at=at)
            route = {name: sb("route_" + name, [P, NT, E], at=at) for name in
                     ("ex", "sc", "oh1", "oh2", "tmp", "both", "cur", "nxt", "pos")}
            row = {name: sb("route_" + name, [P, NT, 1], at=at) for name in ("mx", "sum", "rec", "pick", "s1", "s2")}
            iota_e = sb("iota_e", [P, NT, E], at=at)
            iota_ei = sb("iota_ei", [P, NT, E], I32, at)
            count = {name: sb("route_" + name, [P, 1, E], at=at) for name in ("total", "padded", "end", "end2", "start")}
            count_i = sb("count_i", [P, E], I32, at)
            first_row = sb("first_row", [P, NJ, E], at=at)
            first_row_i = sb("first_row_i", [P, NJ, E], I32, at)
            below = sb("below", [P, NJ, E], at=at)
            eid_f = sb("eid_f", [P, NJ, 1], at=at)
            earlier = sb("earlier", [P, P], at=at)
            ones = sb("ones", [P, P], at=at)
        expert_weights(3, ctx)
        with ExitStack() as at:
            cb_gb = sb("cb_gb", [P, B, D], at=at)
            cb_base = sb("cb_base", [P, 2, D], at=at)
            cb_y1 = sb("cb_y1", [P, 2, D], at=at)
            cb_y2 = sb("cb_y2", [P, 2, D], at=at)
            cb_out = sb("cb_out", [P, 2, D], at=at)
        for i in range(2):
            expert_weights(i, ctx)
        gu_hi, gu_lo, dn_hi, dn_lo = (w[2:] + w[:2] for w in (gu_hi, gu_lo, dn_hi, dn_lo))

        vec_in = sem("vec_in")
        c_in = sem("c_in")
        wmod_in = [sem(f"wmod_in{q}") for q in range(3)]
        u_in = sem("u_in")
        w_in = pair_of_sems("w_in")
        mod_out = sem("mod_out")
        mod1_in = sem("mod1_in")
        mod2_in = sem("mod2_in")
        x_in = pair_of_sems("x_in")
        h_out = pair_of_sems("h_out")
        o_out = pair_of_sems("o_out")
        h_in = pair_of_sems("h_in")
        o_in = pair_of_sems("o_in")
        x2_out = pair_of_sems("x2_out")
        x2_in = pair_of_sems("x2_in")
        xr_in = pair_of_sems("xr_in")
        xres_out = pair_of_sems("xres_out")
        h3_out = pair_of_sems("h3_out")
        zero_out = sem("zero_out")
        raw_in = pair_of_sems("raw_in")
        mod3_in = sem("mod3_in")
        sx_in = pair_of_sems("sx_in")
        sr_in = pair_of_sems("sr_in")
        base_out = pair_of_sems("base_out")
        sc_in = pair_of_sems("sc_in")
        sc_out = pair_of_sems("sc_out")
        ex_in = pair_of_sems("ex_in")
        ys_out = pair_of_sems("ys_out")
        gb_in = sem("gb_in")
        cb_in = pair_of_sems("cb_in")
        y1_in = pair_of_sems("y1_in")
        y2_in = pair_of_sems("y2_in")
        final_out = pair_of_sems("final_out")
        const_pool = sem("const_pool")
        const_ready = sem("const_ready")
        silu_c = sem("silu_c")
        mod_mm = sem("mod_mm")
        mod_vec = sem("mod_vec")
        u_ready = sem("u_ready")
        wsplit_hi = sem("wsplit_hi")
        wsplit_lo = sem("wsplit_lo")
        lnx_vec = steps("lnx_vec", "stats", "moments")
        lnx_pool = steps("lnx_pool", "var", "rstd")
        lnh_vec = steps("lnh_vec", "scaled", "h", "stats", "moments")
        lnh_pool = steps("lnh_pool", "var", "rstd")
        hh_vec = steps("hh_vec", "hhat")
        t1_pe = steps("t1_pe", "turned")
        h1T_act = steps("h1T_act", "h1T")
        mix_act = steps("mix_act", "mix_hi")
        mix_vec = steps("mix_vec", "first_col", "mixed", "mix_lo")
        mix_pool = steps("mix_pool", "diff")
        rkv_pe = steps("rkv_pe", "r", "k", "v")
        sr_act = steps("sr_act", "sr")
        sk_act = steps("sk_act", "sk")
        post_vec = steps("post_vec", "z", "vk")
        rw_pool = steps("rw_pool", "rw")
        rw_pe = steps("rw_pe", "turned", "out")
        rw_act = steps("rw_act", "rw_hi")
        rw_vec = steps("rw_vec", "rw_lo")
        o_act = steps("o_act", "o")
        x2_pool = steps("x2_pool", "x2")
        ln2_vec = steps("ln2_vec", "stats", "moments")
        ln2_pool = steps("ln2_pool", "var", "rstd")
        xh2_vec = steps("xh2_vec", "xhat")
        t2_pe = steps("t2_pe", "turned")
        h2T_act = steps("h2T_act", "h2T")
        mix2_act = steps("mix2_act", "mix_hi")
        mix2_vec = steps("mix2_vec", "first_col", "mixed", "mix_lo")
        mix2_pool = steps("mix2_pool", "diff")
        rk2_pe = steps("rk2_pe", "r2", "k2")
        post2_act = steps("post2_act", "sr2", "relu", "k2")
        tk_pe = steps("tk_pe", "turned", "cv")
        tk_act = steps("tk_act", "k2_hi")
        tk_vec = steps("tk_vec", "k2_lo")
        y_vec = steps("y_vec", "y")
        res_pool = steps("res_pool", "x3", "gated", "xres")
        ln3_vec = steps("ln3_vec", "stats", "moments", "scaled", "h3")
        ln3_pool = steps("ln3_pool", "var", "rstd")
        t3_pe = steps("t3_pe", "turned", "logits")
        t3_act = steps("t3_act", "h3_hi")
        t3_vec = steps("t3_vec", "h3_lo")
        lg_vec = steps("lg_vec", "part", "copied")

        zeroed = sem("zeroed")
        ex_const_i = sem("ex_const_i")
        ex_const = sem("ex_const")
        pad_ready = sem("pad_ready")
        route_vec = sem("route_vec")
        route_exp = sem("route_exp")
        route_pe = sem("route_pe")
        route_done = sem("route_done")
        sh_split_hi = sem("sh_split_hi")
        sh_split_lo = sem("sh_split_lo")
        shx_pe = steps("shx_pe", "turned")
        shx_act = steps("shx_act", "hi")
        shx_vec = steps("shx_vec", "lo")
        shu_pe = Apart(sem, "shu_pe", "up", "turned", "down")
        shu_act = steps("shu_act", "silu", "hid_hi")
        shu_vec = Apart(sem, "shu_vec", "hid", "hid_lo")
        base_vec = steps("base_vec", "gated", "base")
        rx_pe = steps("rx_pe", "turned")
        rx_act = steps("rx_act", "hi")
        rx_vec = steps("rx_vec", "lo")
        ru_pe = Apart(sem, "ru_pe", "up", "turned", "down")
        ru_act = steps("ru_act", "silu", "hid_hi")
        ru_vec = Apart(sem, "ru_vec", "hid", "hid_lo", "y")
        rw_hi_act = steps("rw_hi_act", "gu_hi", "dn_hi")
        rw_lo_vec = steps("rw_lo_vec", "gu_lo", "dn_lo")
        cb_vec = steps("cb_vec", "first", "both", "gated", "out")

        ORDER = W1 + W2
        NW = len(ORDER)

        def product(pe, acc, act_hi, act_lo, w_hi, w_lo):
            chunks = len(act_hi)
            for i in range(chunks):
                pe.matmul(acc, act_hi[i], w_hi[i], start=(i == 0), stop=False)
                pe.matmul(acc, act_hi[i], w_lo[i], start=False, stop=False)
                last = pe.matmul(acc, act_lo[i], w_hi[i], start=False, stop=(i == chunks - 1))
            return last

        def chunks_of(ap, n=C):
            return [ap[:, c, :] for c in range(n)]

        def turn(pe, bank, rows):
            for c in range(C):
                last = pe.transpose(bank[:, c * P:(c + 1) * P], rows[:, c * P:(c + 1) * P], ident[:])
            return last

        def bank_chunks(bank):
            return bank[:].rearrange("p (c t) -> p c t", c=C)

        PS_R, PS_K, PS_O, PS_T1, PS_TR = psum[0:5]
        PS_V = psum[5:7]
        PS_R2, PS_K2, PS_CV, PS_T2, PS_TK, PS_T3, PS_LG = psum[0:7]

        def wait_a1(eng):
            for p in range(2):
                eng.wait_ge(h_out[p], 16 * (NT // 2))
                eng.wait_ge(o_out[p], 16 * (NT // 2))

        MOD_DONE = 14

        CONSTS = 5
        ROUTE_BOTH = 17


        def bridge(dve, which, reached):
            dve.wait_ge(*reached)
            dve.tensor_copy(bridge_col[:, which:which + 1], eps[:])

        def flat_of(weights, t):
            return flat(weights[2 + t.p][:])

        def scatter(pool, n):
            pool.wait_ge(sc_in[n % 2], 16 * (n // 2) + 16)
            for k in range(2):
                pool.indirect_dma_start(xs_d, bass.IndirectOffsetOnAxis(ap=slots[:, k, n:n + 1], axis=0),
                                        sc_t[n % 2], None).then_inc(sc_out[n % 2], 16)

        def load_raw(sp, i, gu_rows, dn_rows):
            whole = FK - 1
            sp.dma_start(raw[i][:, 0:C * GU], gu_rows).then_inc(raw_in[i], 16)
            sp.dma_start(raw[i][:, C * GU:C * GU + whole * D].rearrange("p (k d) -> p k d", k=whole),
                         dn_rows[0:whole * P, :].rearrange("(k p) d -> p k d", p=P)).then_inc(raw_in[i], 16)
            sp.dma_start(raw[i][0:F - whole * P, C * GU + whole * D:RAW], dn_rows[whole * P:F, :]).then_inc(raw_in[i], 16)

        def wait_a2(eng):
            eng.wait_ge(*lg_vec.done(NT - 1, "copied"))
            for p in range(2):
                eng.wait_ge(xres_out[p], 16 * (NT // 2))
                eng.wait_ge(h3_out[p], 16 * (NT // 2))

        def wait_shared(eng):
            for p in range(2):
                eng.wait_ge(base_out[p], 16 * (NT // 2))

        def wait_routed(eng):
            for p in range(2):
                eng.wait_ge(ys_out[p], 16 * NJ)

        PS_X, PS_G, PS_U, PS_H, PS_RT, PS_Y = psum[0], psum[1:3], psum[3:5], psum[5], psum[6], psum[7]
        PS_PRE = PS_RT[:, 0:NT * E].rearrange("p (t e) -> p t e", e=E)
        PS_TOT = PS_RT[:, NT * E:2 * NT * E].rearrange("p (t e) -> p t e", e=E)

        block = ctx.enter_context(nc.Block())

        @block.sync
        def _(sp):
            names = ["ln1_g", "ln1_b", "ln2_g", "ln2_b", "mu_r", "mu_k", "mu_v", "mu_r2", "mu_k2"]

            def load_wmod(q):
                for c in range(C):
                    sp.dma_start(wmod[:, c, 2 * q * D:2 * (q + 1) * D],
                                 io["wmod"][c * P:(c + 1) * P, 2 * q * D:2 * (q + 1) * D]).then_inc(wmod_in[q], 16)

            def load_weight(i):
                if i >= 2:
                    sp.wait_ge(wsplit_lo, i - 1)
                sp.dma_start(stage[i % 2][:].rearrange("p (c n) -> p c n", c=C),
                             io["w_" + ORDER[i]].rearrange("(c p) n -> p c n", p=P)).then_inc(w_in[i % 2], 16)

            sp.dma_start(cT[:], io["cT"].rearrange("(c p) b -> p c b", p=P)).then_inc(c_in, 16)
            load_wmod(0)
            load_weight(0)
            load_weight(1)
            load_wmod(1)
            load_wmod(2)
            for i in range(2, len(W1)):
                load_weight(i)
            sp.dma_start(u_bc[:], io["u"].partition_broadcast(P)).then_inc(u_in, 16)
            sp.dma_start(wrt[:], io["wrT"].rearrange("(c p) e -> p c e", p=P)).then_inc(vec_in, 16)
            for i, name in enumerate(names):
                sp.dma_start(vecs[:, i, :], io[name].rearrange("(c p) -> p c", p=P),
                             allow_slow_non_contiguous=True).then_inc(vec_in, 16)
            for i in range(len(W1), len(W1) + 2):
                load_weight(i)
            sp.wait_ge(mod_vec, MOD_DONE)
            for m in range(6):
                sp.dma_start(mod_d[:, m * D:(m + 1) * D], mod_rows[m]).then_inc(mod_out, 16)
            sp.wait_ge(mod_out, 96)
            for b in range(B):
                sp.dma_start(flat(mod1[:, b]), mod_d[b, 0:2 * D].partition_broadcast(P)).then_inc(mod1_in, 16)
            load_weight(NW - 1)

            def load_x(t):
                row = sp.snap(t.n * P) if t.pair is not None else t.n * P
                if t.back(2).real():
                    sp.wait_ge(*lnh_vec.done(t.back(2).n, "scaled"))
                sp.dma_start(x_t[:, t.p, :], x_d[bass.ds(row, P), :]).then_inc(x_in[t.p], 16)

            def store_h(t):
                row = sp.snap(t.n * P) if t.pair is not None else t.n * P
                sp.wait_ge(*lnh_vec.done(t.n, "h"))
                sp.dma_start(h_d[bass.ds(row, P), :], h_t[:, t.p, :]).then_inc(h_out[t.p], 16)

            def store_o(t):
                row = sp.snap(t.n * P) if t.pair is not None else t.n * P
                sp.wait_ge(*o_act.done(t.n, "o"))
                sp.dma_start(o_d[bass.ds(row, P), :], o_t[:, t.p, :]).then_inc(o_out[t.p], 16)

            def zero_part(t):
                row = sp.snap(t.n * ZERO_ROWS) if t.pair is not None else t.n * ZERO_ROWS
                sp.dma_start(xs_d[bass.ds(row, ZERO_ROWS), :].rearrange("(p r) d -> p r d", r=ZERO_REPEAT),
                             zero_rows[0:ZERO_ROWS // ZERO_REPEAT, :].unsqueeze(1).to_broadcast(
                                 [ZERO_ROWS // ZERO_REPEAT, ZERO_REPEAT, D])).then_inc(zero_out, 16)

            sp.wait_ge(zeroed, 1)
            sweep(sp, NT, *in_turn((store_o, 3), (load_x, -5), (store_h, -3), (zero_part, 0)))

            wait_a1(sp)
            def load_ho(t):
                row = sp.snap(t.n * P) if t.pair is not None else t.n * P
                if t.back(2).real():
                    sp.wait_ge(*x2_pool.done(t.back(2).n, "x2"))
                sp.dma_start(hin_t[:, t.p, :], h_d[bass.ds(row, P), :]).then_inc(h_in[t.p], 16)
                sp.dma_start(oin_t[:, t.p, :], o_d[bass.ds(row, P), :]).then_inc(o_in[t.p], 16)

            def store_x2(t):
                row = sp.snap(t.n * P) if t.pair is not None else t.n * P
                sp.wait_ge(*x2_pool.done(t.n, "x2"))
                sp.dma_start(x2_d[bass.ds(row, P), :], x2_t[:, t.p, :]).then_inc(x2_out[t.p], 16)

            def load_x2(t):
                row = sp.snap(t.n * P) if t.pair is not None else t.n * P
                if t.back(2).real():
                    sp.wait_ge(*res_pool.done(t.back(2).n, "x3"))
                sp.wait_ge(x2_out[t.p], 16 * t.half + 16)
                sp.dma_start(x2r_t[:, t.p, :], x2_d[bass.ds(row, P), :]).then_inc(x2_in[t.p], 16)

            def load_xr(t):
                row = sp.snap(t.n * P) if t.pair is not None else t.n * P
                if t.back(2).real():
                    sp.wait_ge(*ln3_vec.done(t.back(2).n, "scaled"))
                    sp.wait_ge(xres_out[t.p], 16 * t.half)
                sp.dma_start(xr_t[:, t.p, :], x_d[bass.ds(row, P), :]).then_inc(xr_in[t.p], 16)

            def store_xres(t):
                row = sp.snap(t.n * P) if t.pair is not None else t.n * P
                sp.wait_ge(*res_pool.done(t.n, "xres"))
                sp.dma_start(xres_d[bass.ds(row, P), :], xr_t[:, t.p, :]).then_inc(xres_out[t.p], 16)

            def store_h3(t):
                row = sp.snap(t.n * P) if t.pair is not None else t.n * P
                sp.wait_ge(*ln3_vec.done(t.n, "h3"))
                sp.dma_start(h3_d[bass.ds(row, P), :], h3_t[:, t.p, :]).then_inc(h3_out[t.p], 16)

            def load_mod2(t):
                if t.pair is None and t.n == 0:
                    for b in range(B):
                        sp.dma_start(flat(mod2[:, b]), mod_d[b, 2 * D:5 * D].partition_broadcast(P)).then_inc(mod2_in, 16)

            sweep(sp, NT, *in_turn((load_ho, -5), (load_mod2, -2), (load_x2, 1), (store_xres, 2), (load_xr, 1), (store_h3, 3), (store_x2, -4)))

            wait_a2(sp)
            for i in range(2):
                sp.wait_ge(pad_ready, 2)
                load_raw(sp, i, io["sh_gu"][i], io["sh_dn"][i])
            for b in range(B):
                sp.dma_start(mod3[:, b, :], mod_d[b, 5 * D:6 * D].partition_broadcast(P)).then_inc(mod3_in, 16)

            def load_shared(t):
                row_of = sp.snap(t.n * P) if t.pair is not None else t.n * P
                if t.back(2).real():
                    sp.wait_ge(*shx_pe.done(t.back(2).n, "turned"))
                sp.dma_start(ex_x[:, t.p, :], h3_d[bass.ds(row_of, P), :]).then_inc(sx_in[t.p], 16)
                if t.back(2).real():
                    sp.wait_ge(*base_vec.done(t.back(2).n, "base"))
                sp.dma_start(xres_t[:, t.p, :], xres_d[bass.ds(row_of, P), :]).then_inc(sr_in[t.p], 16)

            def store_base(t):
                row_of = sp.snap(t.n * P) if t.pair is not None else t.n * P
                sp.wait_ge(*base_vec.done(t.n, "base"))
                sp.dma_start(base_d[bass.ds(row_of, P), :], base_t[:, t.p, :]).then_inc(base_out[t.p], 16)

            def shared_step(t):
                for stage_of, shift in ((store_base, 2), (load_shared, -2)):
                    st = t.back(shift)
                    if st.real():
                        stage_of(st)

            sweep(sp, NT, 2, 2, shared_step)

            sp.wait_ge(route_done, 1)

            def load_expert(t):
                e = sp.value_load(eid[0:1, bass.ds(t.n, 1)], min_val=0, max_val=E - 1)
                if t.back(2).real():
                    sp.wait_ge(*rw_lo_vec.done(t.back(2).n, "dn_lo"))
                else:
                    sp.wait_ge(sh_split_lo, 4)
                load_raw(sp, t.p, io["ex_gu"][bass.ds(e, 1)].rearrange("a p c -> (a p) c"),
                         io["ex_dn"][bass.ds(e, 1)].rearrange("a f d -> (a f) d"))

            def load_rows(t):
                for half in range(2):
                    u = t.unit(half)
                    row_of = sp.snap(u.n * P) if t.pair is not None else u.n * P
                    if t.back(1).real():
                        sp.wait_ge(*rx_pe.done(u.back(2).n, "turned"))
                    sp.dma_start(ex_x[:, half, :], xs_d[bass.ds(row_of, P), :]).then_inc(ex_in[half], 16)

            for t in (Tile(None, j, NJ) for j in range(2)):
                load_expert(t)
            for p in range(2):
                sp.wait_ge(sc_out[p], 32 * (NT // 2))
            wait_shared(sp)

            def routed_step(t):
                if t.back(-1).real():
                    load_rows(t.back(-1))
                if t.real() and t.back(-2).real():
                    load_expert(t.back(-2))

            sweep(sp, NJ, 2, 0, routed_step)

            wait_routed(sp)
            for b in range(B):
                sp.dma_start(cb_gb[:, b, :], mod_d[b, 5 * D:6 * D].partition_broadcast(P)).then_inc(gb_in, 16)

            def load_base(t):
                row_of = sp.snap(t.n * P) if t.pair is not None else t.n * P
                if t.back(2).real():
                    sp.wait_ge(*cb_vec.done(t.back(2).n, "out"))
                sp.dma_start(cb_base[:, t.p, :], base_d[bass.ds(row_of, P), :]).then_inc(cb_in[t.p], 16)

            def store_out(t):
                row_of = sp.snap(t.n * P) if t.pair is not None else t.n * P
                sp.wait_ge(*cb_vec.done(t.n, "out"))
                sp.dma_start(out_d[bass.ds(row_of, P), :], cb_out[:, t.p, :]).then_inc(final_out[t.p], 16)

            def combine_step(t):
                for stage_of, shift in ((store_out, 1), (load_base, -2)):
                    st = t.back(shift)
                    if st.real():
                        stage_of(st)

            sweep(sp, NT, 2, 1, combine_step)
            for p in range(2):
                sp.wait_ge(final_out[p], 16 * (NT // 2))
            sp.wait_ge(zero_out, 16 * NT)

        @block.gpsimd
        def _(pool):
            pool.memset(ident[:], 0.0).then_inc(const_pool, 1)
            pool.iota(keep_i[:].rearrange("p (t c) -> p t c", c=C), [[0, NT // TPB], [1, TPB], [0, C]], base=0,
                      channel_multiplier=0).then_inc(const_pool, 1)
            pool.memset(zero_rows[:], 0.0).then_inc(zeroed, 1)
            pool.memset(eps[:], EPS).then_inc(const_ready, 1)
            pool.memset(minus_half[:], -0.5).then_inc(const_ready, 1)
            pool.memset(h1T[:, 1, :, P:P + 1], 0.0).then_inc(const_ready, 1)
            pool.wait_ge(const_pool, 2)
            pool.affine_select(out=ident[:], in_=ident[:], compare_op=ALU.not_equal, fill=1.0, base=0,
                               pattern=[[-1, P]], channel_multiplier=1).then_inc(const_ready, 1)
            pool.tensor_scalar(keep[:], keep_i[:], 0.0, None, ALU.is_gt).then_inc(const_ready, 1)
            pool.wait_ge(const_ready, CONSTS)

            def x_rstd(t):
                pool.wait_ge(*lnx_vec.done(t.n, "moments"))
                pool.tensor_tensor(var1[:, 0:1], mv1[:, t.p, 1:2], eps[:], ALU.add).then_inc(lnx_pool.sem, 1)
                pool.wait_ge(*lnx_pool.done(t.n, "var"))
                pool.tensor_tensor(rstd1[:, t.p, :], var1[:, 0:1], minus_half[:], ALU.pow).then_inc(lnx_pool.sem, 1)

            def h_rstd(t):
                pool.wait_ge(*lnh_vec.done(t.n, "moments"))
                pool.tensor_tensor(var1[:, 1:2], mv1h[:, t.p, 1:2], eps[:], ALU.add).then_inc(lnh_pool.sem, 1)
                pool.wait_ge(*lnh_pool.done(t.n, "var"))
                pool.tensor_tensor(rstd1h[:, t.p, :], var1[:, 1:2], minus_half[:], ALU.pow).then_inc(lnh_pool.sem, 1)

            def diff(t):
                pool.wait_ge(*h1T_act.done(t.n, "h1T"))
                pool.wait_ge(*mix_vec.done(t.n, "first_col"))
                pool.tensor_tensor(diff1[:], h1T[:, t.p, :, 1:P + 1], h1T[:, t.p, :, 0:P],
                                   ALU.subtract).then_inc(mix_pool.sem, 1)

            def rw(t):
                pool.wait_ge(*sr_act.done(t.n, "sr"))
                pool.wait_ge(*post_vec.done(t.n, "vk"))
                if t.back(1).real():
                    pool.wait_ge(*rw_pe.done(t.back(1).n, "turned"))
                pool.tensor_tensor(rw_t, vk_t, sr_t[t.p], ALU.mult).then_inc(rw_pool.sem, 1)

            sweep(pool, NT, *in_turn((diff, -1), (x_rstd, -4), (rw, 1), (h_rstd, -3)))

            wait_a1(pool)
            pool.memset(h2T[:, 1, :, P:P + 1], 0.0).then_inc(const_ready, 1)

            def x2(t):
                if t.back(2).real():
                    pool.wait_ge(*xh2_vec.done(t.back(2).n, "xhat"))
                    pool.wait_ge(x2_out[t.p], 16 * t.half)
                pool.wait_ge(h_in[t.p], 16 * t.half + 16)
                pool.wait_ge(o_in[t.p], 16 * t.half + 16)
                pool.tensor_tensor(x2_t[:, t.p, :], hin_t[:, t.p, :], oin_t[:, t.p, :], ALU.add).then_inc(x2_pool.sem, 1)

            def rstd_2(t):
                pool.wait_ge(*ln2_vec.done(t.n, "moments"))
                pool.tensor_tensor(var2[:, 0:1], mv2[:, t.p, 1:2], eps[:], ALU.add).then_inc(ln2_pool.sem, 1)
                pool.wait_ge(*ln2_pool.done(t.n, "var"))
                pool.tensor_tensor(rstd2[:, t.p, :], var2[:, 0:1], minus_half[:], ALU.pow).then_inc(ln2_pool.sem, 1)

            def diff_2(t):
                pool.wait_ge(*h2T_act.done(t.n, "h2T"))
                pool.wait_ge(*mix2_vec.done(t.n, "first_col"))
                pool.tensor_tensor(diff2[:], h2T[:, t.p, :, 1:P + 1], h2T[:, t.p, :, 0:P],
                                   ALU.subtract).then_inc(mix2_pool.sem, 1)

            def x3(t):
                pool.wait_ge(x2_in[t.p], 16 * t.half + 16)
                pool.wait_ge(*y_vec.done(t.n, "y"))
                pool.tensor_tensor(y_t[:], y_t[:], x2r_t[:, t.p, :], ALU.add).then_inc(res_pool.sem, 1)

            def gated(t):
                batch = t.n // TPB
                if t.pair is None and t.n == 0:
                    pool.wait_ge(mod2_in, 16 * B)
                pool.wait_ge(*res_pool.done(t.n, "x3"))
                pool.tensor_tensor(pool_col[:], eps[:], eps[:], ALU.add)
                pool.tensor_tensor(y_t[:], y_t[:], mod2[:, bass.ds(batch, 1), 0, :].rearrange("p a d -> p (a d)"),
                                   ALU.mult).then_inc(res_pool.sem, 1)

            def xres(t):
                pool.wait_ge(xr_in[t.p], 16 * t.half + 16)
                pool.wait_ge(*res_pool.done(t.n, "gated"))
                pool.tensor_tensor(xr_t[:, t.p, :], xr_t[:, t.p, :], y_t[:], ALU.add).then_inc(res_pool.sem, 1)

            def rstd_3(t):
                pool.wait_ge(*ln3_vec.done(t.n, "moments"))
                pool.tensor_tensor(var2[:, 1:2], mv3[:, t.p, 1:2], eps[:], ALU.add).then_inc(ln3_pool.sem, 1)
                pool.wait_ge(*ln3_pool.done(t.n, "var"))
                pool.tensor_tensor(rstd3[:, t.p, :], var2[:, 1:2], minus_half[:], ALU.pow).then_inc(ln3_pool.sem, 1)

            sweep(pool, NT, *in_turn((diff_2, -1), (x3, 2), (rstd_3, 3), (rstd_2, -3), (gated, 2), (xres, 2), (x2, -4)))

            wait_a2(pool)
            pool.iota(iota_ei[:], [[0, NT], [1, E]], base=-E, channel_multiplier=0).then_inc(ex_const_i, 1)
            pool.iota(first_row_i[:], [[R, NJ], [0, E]], base=0, channel_multiplier=0).then_inc(ex_const_i, 1)
            pool.memset(ones[:], 1.0).then_inc(ex_const_i, 1)
            pool.wait_ge(ex_const_i, 3)
            pool.tensor_copy(iota_e[:], iota_ei[:]).then_inc(ex_const, 1)
            pool.tensor_copy(first_row[:], first_row_i[:]).then_inc(ex_const, 1)
            pool.affine_select(out=earlier[:], in_=ones[:], compare_op=ALU.is_gt, fill=0.0, base=0,
                               pattern=[[1, P]], channel_multiplier=-1).then_inc(ex_const, 1)

            pool.wait_ge(route_done, 1)
            pool.wait_ge(zero_out, 16 * NT)
            for n in range(NT):
                if n >= 2:
                    pool.wait_ge(sc_out[n % 2], 32 * (n // 2))
                pool.dma_start(sc_t[n % 2], h3_d[n * P:(n + 1) * P, :]).then_inc(sc_in[n % 2], 16)
                if n >= 1:
                    scatter(pool, n - 1)
            scatter(pool, NT - 1)

            wait_routed(pool)
            for n in range(NT):
                if n >= 2:
                    pool.wait_ge(*cb_vec.done(n - 2, "both"))
                for k, (rows, arrived) in enumerate(((cb_y1, y1_in), (cb_y2, y2_in))):
                    pool.indirect_dma_start(rows[:, n % 2, :], None, ys_d,
                                            bass.IndirectOffsetOnAxis(ap=slots[:, k, n:n + 1], axis=0)
                                            ).then_inc(arrived[n % 2], 16)

        @block.scalar
        def _(act):
            act.wait_ge(c_in, 16)
            act.activation(cT[:], cT[:], ACT.Silu).then_inc(silu_c, 1)
            for i, w in enumerate(ORDER):
                act.wait_ge(w_in[i % 2], 16 * (i // 2) + 16)
                if w == W2[0]:
                    act.wait_ge(mod_mm, 6)
                act.activation(flat(hi[w][:]), stage[i % 2][:], ACT.Copy).then_inc(wsplit_hi, 1)
            act.wait_ge(vec_in, 160)
            act.activation(wrt_hi, wrt[:], ACT.Copy).then_inc(wsplit_hi, 1)

            def h1T_of(t):
                act.wait_ge(*t1_pe.done(t.n, "turned"))
                if t.back(1).real():
                    act.wait_ge(*mix_vec.done(t.back(1).n, "first_col"))
                for c in range(C):
                    last = act.activation(h1T[:, t.p, c, 1:P + 1], PS_T1[:, c * P:(c + 1) * P], ACT.Identity,
                                          bias=vecs[:, B1, c:c + 1], scale=vecs[:, G1, c:c + 1])
                last.then_inc(h1T_act.sem, 1)

            def mix_hi(t):
                if t.back(2).real():
                    act.wait_ge(*rkv_pe.done(t.back(2).n, "v"))
                act.wait_ge(*mix_vec.done(t.n, "mixed"))
                act.activation(xm_hi[:, t.p].rearrange("p m c t -> p (m c t)"), stage[0][:, 0:3 * D],
                               ACT.Copy).then_inc(mix_act.sem, 1)

            def sr(t):
                if t.back(2).real():
                    act.wait_ge(*rw_pool.done(t.back(2).n, "rw"))
                act.wait_ge(*rkv_pe.done(t.n, "r"))
                act.activation(sr_t[t.p], PS_R[:], ACT.Sigmoid).then_inc(sr_act.sem, 1)

            def sk(t):
                act.wait_ge(*post_vec.done(t.n, "z"))
                act.activation(sk_t, z_t, ACT.Sigmoid).then_inc(sk_act.sem, 1)

            def rwhi(t):
                if t.back(1).real():
                    act.wait_ge(*rw_pe.done(t.back(1).n, "out"))
                act.wait_ge(*rw_pe.done(t.n, "turned"))
                act.activation(flat(rw_hi[:]), PS_TR[:], ACT.Copy).then_inc(rw_act.sem, 1)

            def o_rows(t):
                if t.back(2).real():
                    act.wait_ge(o_out[t.p], 16 * t.half)
                act.wait_ge(*rw_pe.done(t.n, "out"))
                act.activation(o_t[:, t.p, :], PS_O[:], ACT.Copy).then_inc(o_act.sem, 1)

            sweep(act, NT, *in_turn((o_rows, 3), (sk, 1), (sr, 0), (rwhi, 2), (mix_hi, -1), (h1T_of, -2)))

            wait_a1(act)

            def h2T_of(t):
                act.wait_ge(*t2_pe.done(t.n, "turned"))
                if t.back(1).real():
                    act.wait_ge(*mix2_vec.done(t.back(1).n, "first_col"))
                for c in range(C):
                    last = act.activation(h2T[:, t.p, c, 1:P + 1], PS_T2[:, c * P:(c + 1) * P], ACT.Identity,
                                          bias=vecs[:, B2, c:c + 1], scale=vecs[:, G2, c:c + 1])
                last.then_inc(h2T_act.sem, 1)

            def mix2_hi(t):
                if t.back(2).real():
                    act.wait_ge(*rk2_pe.done(t.back(2).n, "k2"))
                act.wait_ge(*mix2_vec.done(t.n, "mixed"))
                act.activation(xm2_hi[:, t.p].rearrange("p m c t -> p (m c t)"), mix2[:].rearrange("p m c t -> p (m c t)"),
                               ACT.Copy).then_inc(mix2_act.sem, 1)

            def sr2_of(t):
                if t.back(2).real():
                    act.wait_ge(*y_vec.done(t.back(2).n, "y"))
                act.wait_ge(*rk2_pe.done(t.n, "r2"))
                act.activation(sr2[:, t.p, :], PS_R2[:], ACT.Sigmoid).then_inc(post2_act.sem, 1)

            def k2_of(t):
                if t.back(1).real():
                    act.wait_ge(*tk_pe.done(t.back(1).n, "turned"))
                act.wait_ge(*rk2_pe.done(t.n, "k2"))
                act.activation(k2_t[:], PS_K2[:], ACT.Relu).then_inc(post2_act.sem, 1)
                act.wait_ge(*post2_act.done(t.n, "relu"))
                act.activation(k2_t[:], k2_t[:], ACT.Square).then_inc(post2_act.sem, 1)

            def k2hi(t):
                if t.back(1).real():
                    act.wait_ge(*tk_pe.done(t.back(1).n, "cv"))
                act.wait_ge(*tk_pe.done(t.n, "turned"))
                act.activation(flat(k2_hi[:]), PS_TK[:], ACT.Copy).then_inc(tk_act.sem, 1)

            def h3hi(t):
                if t.back(1).real():
                    act.wait_ge(*t3_pe.done(t.back(1).n, "logits"))
                act.wait_ge(*t3_pe.done(t.n, "turned"))
                act.activation(flat(h3_hi[:]), PS_T3[:], ACT.Copy).then_inc(t3_act.sem, 1)

            sweep(act, NT, *in_turn((sr2_of, 0), (k2hi, 1), (h3hi, 4), (mix2_hi, -1), (k2_of, 0), (h2T_of, -2)))

            wait_a2(act)
            act.wait_ge(route_vec, 2)
            act.activation(route["ex"][:], route["ex"][:], ACT.Exp).then_inc(route_exp, 1)
            for i in range(2):
                act.wait_ge(raw_in[i], 48)
                act.activation(flat(gu_hi[i][:]), raw[i][:, 0:C * GU], ACT.Copy).then_inc(sh_split_hi, 1)
                act.activation(flat(dn_hi[i][:]), raw[i][:, C * GU:RAW], ACT.Copy).then_inc(sh_split_hi, 1)

            def hidhi(u, first, pe_steps, act_steps):
                if not first:
                    act.wait_ge(*pe_steps.done(u.back(1).n, "down"))
                act.wait_ge(*pe_steps.done(u.n, "turned"))
                act.activation(flat(hid_hi[:]), PS_H[:, 0:FK * P], ACT.Copy).then_inc(act_steps.sem, 1)

            def silu(u, first, pe_steps, act_steps, vec_steps):
                if not first:
                    act.wait_ge(*vec_steps.done(u.back(1).n, "hid"))
                act.wait_ge(*pe_steps.done(u.n, "up"))
                act.activation(sg_t[:], PS_G[u.half][:, 0:F], ACT.Silu).then_inc(act_steps.sem, 1)

            def shared_x_hi(t):
                if t.back(2).real():
                    act.wait_ge(*shu_pe.done(t.back(2).unit(1).n, "up"))
                act.wait_ge(*shx_pe.done(t.n, "turned"))
                act.activation(flat(ex_x_hi[:, t.p]), PS_X[:], ACT.Copy).then_inc(shx_act.sem, 1)

            def shared_step(t):
                if t.back(-1).real():
                    shared_x_hi(t.back(-1))
                for half in range(2):
                    before = t if half else t.back(1)
                    if before.real():
                        u = before.unit(1 - half)
                        hidhi(u, not before.back(1).real() and half, shu_pe, shu_act)
                    if t.real():
                        silu(t.unit(half), not t.back(1).real() and not half, shu_pe, shu_act, shu_vec)

            sweep(act, NT, 1, 1, shared_step)

            wait_shared(act)
            act.wait_ge(sc_out[0], 32 * (NT // 2))
            act.wait_ge(sc_out[1], 32 * (NT // 2))

            def expert_hi(t, part):
                if part == 0:
                    if t.back(2).real():
                        act.wait_ge(*ru_pe.done(t.back(2).unit(1).n, "up"))
                    act.wait_ge(raw_in[t.p], 48 * t.half + 96)
                    act.activation(flat_of(gu_hi, t), raw[t.p][:, 0:C * GU], ACT.Copy).then_inc(rw_hi_act.sem, 1)
                else:
                    if t.back(2).real():
                        act.wait_ge(*ru_pe.done(t.back(2).unit(1).n, "down"))
                    act.activation(flat_of(dn_hi, t), raw[t.p][:, C * GU:RAW], ACT.Copy).then_inc(rw_hi_act.sem, 1)

            def routed_x_hi(u, first):
                if not first:
                    act.wait_ge(*ru_pe.done(u.back(2).n, "up"))
                act.wait_ge(*rx_pe.done(u.n, "turned"))
                act.activation(flat(ex_x_hi[:, u.half]), PS_X[:], ACT.Copy).then_inc(rx_act.sem, 1)

            def store_y(t, half):
                u = t.unit(half)
                row_of = act.snap(u.n * P) if t.pair is not None else u.n * P
                act.wait_ge(*ru_vec.done(u.n, "y"))
                act.dma_start(ys_d[bass.ds(row_of, P), :], y_rows[:, half, :]).then_inc(ys_out[half], 16)

            def routed_step(t):
                for half in range(2):
                    before = t if half else t.back(1)
                    after = t.back(-1) if half else t
                    if t.back(-1).real():
                        expert_hi(t.back(-1), half)
                    if half and t.back(-1).real():
                        routed_x_hi(t.back(-1).unit(0), not t.real())
                    if not half and t.real():
                        routed_x_hi(t.unit(1), not t.back(1).real())
                    if before.real():
                        hidhi(before.unit(1 - half), not before.back(1).real() and half, ru_pe, ru_act)
                    if t.real():
                        silu(t.unit(half), not t.back(1).real() and not half, ru_pe, ru_act, ru_vec)
                    if t.back(1).real():
                        store_y(t.back(1), half)

            sweep(act, NJ, 1, 1, routed_step)

        @block.vector
        def _(dve):
            def split_lo(i):
                w = ORDER[i]
                dve.wait_ge(wsplit_hi, i + 1)
                dve.tensor_tensor(flat(lo[w][:]), stage[i % 2][:], flat(hi[w][:]).bitcast(F32),
                                  ALU.subtract).then_inc(wsplit_lo, 1)

            for i in range(len(W1)):
                split_lo(i)
            SA, CA, GA, SB, CB, GB = range(6)
            MOD_ORDER = [SA, CA, SB, CB, GA, GB]
            step = 0
            for i, m in enumerate(MOD_ORDER):
                dve.wait_ge(mod_mm, 6)
                if m in (GA, GB):
                    dve.wait_ge(mod_vec, step)
                    dve.tensor_scalar(gate_sign, psum[m][0:B, :], 0.0, 2.0, ALU.is_ge, ALU.mult).then_inc(mod_vec, 1)
                    dve.tensor_scalar(gate_neg, psum[m][0:B, :], -1.0, 0.25, ALU.mult, ALU.max).then_inc(mod_vec, 1)
                    dve.wait_ge(mod_vec, step + 2)
                    dve.tensor_scalar(gate_sign, gate_sign, -1.0, None, ALU.add).then_inc(mod_vec, 1)
                    dve.tensor_tensor(gate_neg, psum[m][0:B, :], gate_neg, ALU.max).then_inc(mod_vec, 1)
                    dve.wait_ge(mod_vec, step + 4)
                    dve.tensor_tensor(mod_rows[m], gate_sign, gate_neg, ALU.mult).then_inc(mod_vec, 1)
                    step += 5
                else:
                    dve.tensor_scalar(mod_rows[m], psum[m][0:B, :], 1.0 if m in (CA, CB) else 0.0, None,
                                      ALU.add).then_inc(mod_vec, 1)
                    step += 1
            assert step == MOD_DONE
            for i in range(len(W1), NW):
                split_lo(i)
            dve.wait_ge(wsplit_hi, NW + 1)
            dve.tensor_tensor(wrt_lo, wrt[:], wrt_hi.bitcast(F32), ALU.subtract).then_inc(wsplit_lo, 1)
            dve.wait_ge(u_in, 16)
            dve.tensor_scalar(u_bc[:], u_bc[:], LN_1E8, None, ALU.add).then_inc(u_ready, 1)
            dve.wait_ge(const_ready, CONSTS)
            dve.wait_ge(mod1_in, 16 * B)
            dve.wait_ge(u_ready, 1)

            def x_stats(t):
                dve.wait_ge(x_in[t.p], 16 * t.half + 16)
                dve.bn_stats(st1[:, t.p, :], x_t[:, t.p, :]).then_inc(lnx_vec.sem, 1)

            def x_moments(t):
                bridge(dve, 0, lnx_vec.done(t.n, "stats"))
                dve.bn_aggr(mv1[:, t.p, :], st1[:, t.p, :]).then_inc(lnx_vec.sem, 1)

            def scaled(t):
                batch = t.n // TPB
                dve.wait_ge(*lnx_vec.done(t.n, "moments"))
                dve.scalar_tensor_tensor(xh[:], x_t[:, t.p, :], mv1[:, t.p, 0:1],
                                         mod1[:, bass.ds(batch, 1), 1, :].rearrange("p a d -> p (a d)"), ALU.subtract,
                                         ALU.mult).then_inc(lnh_vec.sem, 1)

            def h_of(t):
                batch = t.n // TPB
                if t.back(2).real():
                    dve.wait_ge(h_out[t.p], 16 * t.half)
                dve.wait_ge(*lnx_pool.done(t.n, "rstd"))
                dve.wait_ge(*lnh_vec.done(t.n, "scaled"))
                dve.scalar_tensor_tensor(h_t[:, t.p, :], xh[:], rstd1[:, t.p, :],
                                         mod1[:, bass.ds(batch, 1), 0, :].rearrange("p a d -> p (a d)"), ALU.mult,
                                         ALU.add).then_inc(lnh_vec.sem, 1)

            def h_stats(t):
                dve.wait_ge(*lnh_vec.done(t.n, "h"))
                dve.bn_stats(st1h[:, t.p, :], h_t[:, t.p, :]).then_inc(lnh_vec.sem, 1)

            def h_moments(t):
                bridge(dve, 1, lnh_vec.done(t.n, "stats"))
                dve.bn_aggr(mv1h[:, t.p, :], st1h[:, t.p, :]).then_inc(lnh_vec.sem, 1)

            def hhat(t):
                if t.back(2).real():
                    dve.wait_ge(*t1_pe.done(t.back(2).n, "turned"))
                dve.wait_ge(*lnh_pool.done(t.n, "rstd"))
                dve.tensor_scalar(hh[:, t.p, :], h_t[:, t.p, :], mv1h[:, t.p, 0:1], rstd1h[:, t.p, :], ALU.subtract,
                                  ALU.mult).then_inc(hh_vec.sem, 1)

            def first_col(t):
                if t.back(1).real():
                    dve.wait_ge(*h1T_act.done(t.back(1).n, "h1T"))
                dve.tensor_tensor(h1T[:, t.p, :, 0:1], h1T[:, 1 - t.p, :, P:P + 1],
                                  keep[:, bass.ds(t.n * C, C)].unsqueeze(2), ALU.mult).then_inc(mix_vec.sem, 1)

            def mixes(t):
                if t.back(1).real():
                    dve.wait_ge(*mix_act.done(t.back(1).n, "mix_hi"))
                dve.wait_ge(*mix_pool.done(t.n, "diff"))
                for m, mu in enumerate((MUR, MUK, MUV)):
                    for c in range(C):
                        last = dve.scalar_tensor_tensor(mix1[:, m, c, :], diff1[:, c, :], vecs[:, mu, c:c + 1],
                                                        h1T[:, t.p, c, 0:P], ALU.mult, ALU.add)
                last.then_inc(mix_vec.sem, 1)

            def mix_lo(t):
                dve.wait_ge(*mix_act.done(t.n, "mix_hi"))
                dve.tensor_tensor(xm_lo[:, t.p].rearrange("p m c t -> p (m c t)"), stage[0][:, 0:3 * D],
                                  xm_hi[:, t.p].rearrange("p m c t -> p (m c t)").bitcast(F32),
                                  ALU.subtract).then_inc(mix_vec.sem, 1)

            def z_of(t):
                if t.back(1).real():
                    dve.wait_ge(*sk_act.done(t.back(1).n, "sk"))
                dve.wait_ge(*rkv_pe.done(t.n, "k"))
                dve.tensor_tensor(z_t, PS_K[:], u_bc[:], ALU.add).then_inc(post_vec.sem, 1)

            def vk_of(t):
                dve.wait_ge(*rkv_pe.done(t.n, "v"))
                if t.back(1).real():
                    dve.wait_ge(*rw_pool.done(t.back(1).n, "rw"))
                dve.wait_ge(*sk_act.done(t.n, "sk"))
                dve.tensor_tensor(vk_t, PS_V[t.p][:], sk_t, ALU.mult).then_inc(post_vec.sem, 1)

            def rwlo(t):
                dve.wait_ge(*rw_act.done(t.n, "rw_hi"))
                dve.tensor_tensor(flat(rw_lo[:]), PS_TR[:], flat(rw_hi[:]).bitcast(F32),
                                  ALU.subtract).then_inc(rw_vec.sem, 1)

            sweep(dve, NT, *in_turn((first_col, -1), (z_of, 1), (x_stats, -4), (scaled, -3), (hhat, -2), (h_of, -3),
                                    (x_moments, -4), (mixes, -1), (h_stats, -3), (vk_of, 1), (rwlo, 2), (h_moments, -3),
                                    (mix_lo, -1)))

            wait_a1(dve)
            dve.wait_ge(const_ready, CONSTS + 1)

            def stats_2(t):
                dve.wait_ge(*x2_pool.done(t.n, "x2"))
                dve.bn_stats(st2[:, t.p, :], x2_t[:, t.p, :]).then_inc(ln2_vec.sem, 1)

            def moments_2(t):
                bridge(dve, 2, ln2_vec.done(t.n, "stats"))
                dve.bn_aggr(mv2[:, t.p, :], st2[:, t.p, :]).then_inc(ln2_vec.sem, 1)

            def xhat_2(t):
                if t.back(2).real():
                    dve.wait_ge(*t2_pe.done(t.back(2).n, "turned"))
                dve.wait_ge(*ln2_pool.done(t.n, "rstd"))
                dve.tensor_scalar(xh2[:, t.p, :], x2_t[:, t.p, :], mv2[:, t.p, 0:1], rstd2[:, t.p, :], ALU.subtract,
                                  ALU.mult).then_inc(xh2_vec.sem, 1)

            def first_col_2(t):
                if t.back(1).real():
                    dve.wait_ge(*h2T_act.done(t.back(1).n, "h2T"))
                dve.tensor_tensor(h2T[:, t.p, :, 0:1], h2T[:, 1 - t.p, :, P:P + 1],
                                  keep[:, bass.ds(t.n * C, C)].unsqueeze(2), ALU.mult).then_inc(mix2_vec.sem, 1)

            def mixes_2(t):
                if t.back(1).real():
                    dve.wait_ge(*mix2_act.done(t.back(1).n, "mix_hi"))
                dve.wait_ge(*mix2_pool.done(t.n, "diff"))
                for m, mu in enumerate((MUR2, MUK2)):
                    for c in range(C):
                        last = dve.scalar_tensor_tensor(mix2[:, m, c, :], diff2[:, c, :], vecs[:, mu, c:c + 1],
                                                        h2T[:, t.p, c, 0:P], ALU.mult, ALU.add)
                last.then_inc(mix2_vec.sem, 1)

            def mix_lo_2(t):
                dve.wait_ge(*mix2_act.done(t.n, "mix_hi"))
                dve.tensor_tensor(xm2_lo[:, t.p].rearrange("p m c t -> p (m c t)"),
                                  mix2[:].rearrange("p m c t -> p (m c t)"),
                                  xm2_hi[:, t.p].rearrange("p m c t -> p (m c t)").bitcast(F32),
                                  ALU.subtract).then_inc(mix2_vec.sem, 1)

            def k2lo(t):
                dve.wait_ge(*tk_act.done(t.n, "k2_hi"))
                dve.tensor_tensor(flat(k2_lo[:]), PS_TK[:], flat(k2_hi[:]).bitcast(F32),
                                  ALU.subtract).then_inc(tk_vec.sem, 1)

            def y_of(t):
                if t.back(1).real():
                    dve.wait_ge(*res_pool.done(t.back(1).n, "xres"))
                dve.wait_ge(*tk_pe.done(t.n, "cv"))
                dve.wait_ge(*post2_act.done(t.n, "sr2"))
                dve.tensor_tensor(y_t[:], PS_CV[:], sr2[:, t.p, :], ALU.mult).then_inc(y_vec.sem, 1)

            def stats_3(t):
                dve.wait_ge(*res_pool.done(t.n, "xres"))
                dve.bn_stats(st3[:, t.p, :], xr_t[:, t.p, :]).then_inc(ln3_vec.sem, 1)

            def moments_3(t):
                bridge(dve, 3, ln3_vec.done(t.n, "stats"))
                dve.bn_aggr(mv3[:, t.p, :], st3[:, t.p, :]).then_inc(ln3_vec.sem, 1)

            def scaled_3(t):
                batch = t.n // TPB
                if t.back(2).real():
                    dve.wait_ge(h3_out[t.p], 16 * t.half)
                    dve.wait_ge(*t3_pe.done(t.back(2).n, "turned"))
                if t.pair is None and t.n == 0:
                    dve.wait_ge(mod2_in, 16 * B)
                dve.wait_ge(*ln3_vec.done(t.n, "moments"))
                dve.scalar_tensor_tensor(h3_t[:, t.p, :], xr_t[:, t.p, :], mv3[:, t.p, 0:1],
                                         mod2[:, bass.ds(batch, 1), 2, :].rearrange("p a d -> p (a d)"), ALU.subtract,
                                         ALU.mult).then_inc(ln3_vec.sem, 1)

            def h3_of(t):
                batch = t.n // TPB
                dve.wait_ge(*ln3_pool.done(t.n, "rstd"))
                dve.wait_ge(*ln3_vec.done(t.n, "scaled"))
                dve.scalar_tensor_tensor(h3_t[:, t.p, :], h3_t[:, t.p, :], rstd3[:, t.p, :],
                                         mod2[:, bass.ds(batch, 1), 1, :].rearrange("p a d -> p (a d)"), ALU.mult,
                                         ALU.add).then_inc(ln3_vec.sem, 1)

            def h3lo(t):
                dve.wait_ge(*t3_act.done(t.n, "h3_hi"))
                dve.tensor_tensor(flat(h3_lo[:]), PS_T3[:], flat(h3_hi[:]).bitcast(F32),
                                  ALU.subtract).then_inc(t3_vec.sem, 1)

            def logits_out(t):
                dve.wait_ge(*t3_pe.done(t.n, "logits"))
                dve.tensor_scalar(lg_part[:, t.p, :], PS_LG[:, 0:8], 1.0, None, ALU.mult).then_inc(lg_vec.sem, 1)
                dve.wait_ge(*lg_vec.done(t.n, "part"))
                dve.tensor_tensor(logits[:, bass.ds(t.n, 1), :].rearrange("p a e -> p (a e)"), lg_part[:, t.p, :],
                                  PS_LG[:, 8:16], ALU.add).then_inc(lg_vec.sem, 1)

            sweep(dve, NT, *in_turn((y_of, 2), (logits_out, 5), (first_col_2, -1), (stats_3, 3), (stats_2, -3), (moments_3, 3), (xhat_2, -2),
                                    (moments_2, -3), (mixes_2, -1), (scaled_3, 3), (k2lo, 1), (h3lo, 4), (mix_lo_2, -1),
                                    (h3_of, 3)))

            wait_a2(dve)
            for i in range(2):
                dve.memset(raw[i][F % P:P, RAW - D:RAW], 0.0).then_inc(pad_ready, 1)
            dve.memset(hid[:, :, F:FK * P], 0.0).then_inc(pad_ready, 1)
            taken = [0]

            def link(instruction):
                taken[0] += 1
                instruction.then_inc(route_vec, 1)
                dve.wait_ge(route_vec, taken[0])

            def over_e(ap):
                return ap.to_broadcast([P, NT, E])

            link(dve.tensor_reduce(row["mx"][:, :, 0], logits[:], AX.X, ALU.max))
            link(dve.tensor_tensor(route["ex"][:], logits[:], over_e(row["mx"][:]), ALU.subtract))
            dve.wait_ge(route_exp, 1)
            link(dve.tensor_reduce(row["sum"][:, :, 0], route["ex"][:], AX.X, ALU.add))
            link(dve.reciprocal(row["rec"][:], row["sum"][:]))
            link(dve.tensor_tensor(route["sc"][:], route["ex"][:], over_e(row["rec"][:]), ALU.mult))
            dve.wait_ge(ex_const, 3)
            for w, hot in ((w1, "oh1"), (w2, "oh2")):
                link(dve.tensor_reduce(w[:, :, 0], route["sc"][:], AX.X, ALU.max))
                link(dve.tensor_tensor(route["tmp"][:], route["sc"][:], over_e(w[:]), ALU.is_equal))
                link(dve.tensor_tensor(route["tmp"][:], route["tmp"][:], iota_e[:], ALU.mult))
                link(dve.tensor_reduce(row["pick"][:, :, 0], route["tmp"][:], AX.X, ALU.min))
                link(dve.tensor_tensor(route[hot][:], iota_e[:], over_e(row["pick"][:]), ALU.is_equal))
                if hot == "oh1":
                    link(dve.scalar_tensor_tensor(flat(route["sc"][:]), flat(route["oh1"][:]), -2.0, flat(route["sc"][:]),
                                                  ALU.mult, ALU.add))
            link(dve.tensor_tensor(route["both"][:], route["oh1"][:], route["oh2"][:], ALU.add))
            assert taken[0] == ROUTE_BOTH
            dve.wait_ge(route_pe, 1)
            link(dve.tensor_copy(route["cur"][:], PS_TOT))
            cur, nxt = "cur", "nxt"
            s = 1
            while s < NT:
                link(dve.tensor_copy(route[nxt][:, 0:s, :], route[cur][:, 0:s, :]))
                link(dve.tensor_tensor(route[nxt][:, s:NT, :], route[cur][:, s:NT, :], route[cur][:, 0:NT - s, :], ALU.add))
                cur, nxt = nxt, cur
                s *= 2
            link(dve.tensor_copy(count["total"][:], route[cur][:, NT - 1:NT, :]))
            link(dve.tensor_tensor(route["pos"][:], route[cur][:], PS_TOT, ALU.subtract))
            link(dve.tensor_tensor(route["pos"][:], route["pos"][:], PS_PRE, ALU.add))
            link(dve.tensor_scalar(count_i[:], flat(count["total"][:]), float(R - 1), None, ALU.add))
            link(dve.tensor_scalar(count_i[:], count_i[:], -R, None, ALU.bitwise_and))
            link(dve.tensor_copy(flat(count["padded"][:]), count_i[:]))
            link(dve.tensor_copy(count["end"][:], count["padded"][:]))
            cur, nxt = "end", "end2"
            s = 1
            while s < E:
                link(dve.tensor_copy(count[nxt][:, :, 0:s], count[cur][:, :, 0:s]))
                link(dve.tensor_tensor(count[nxt][:, :, s:E], count[cur][:, :, s:E], count[cur][:, :, 0:E - s], ALU.add))
                cur, nxt = nxt, cur
                s *= 2
            link(dve.tensor_tensor(count["start"][:], count[cur][:], count["padded"][:], ALU.subtract))
            link(dve.tensor_tensor(route["pos"][:], route["pos"][:], count["start"][:].to_broadcast([P, NT, E]), ALU.add))
            for k, hot in enumerate(("oh1", "oh2")):
                link(dve.tensor_tensor(route["tmp"][:], route[hot][:], route["pos"][:], ALU.mult))
                link(dve.tensor_reduce(row["s1"][:, :, 0], route["tmp"][:], AX.X, ALU.add))
                link(dve.tensor_copy(slots[:, k, :], row["s1"][:, :, 0]))
            link(dve.tensor_tensor(below[:], count[cur][:].to_broadcast([P, NJ, E]), first_row[:], ALU.is_le))
            link(dve.tensor_reduce(eid_f[:, :, 0], below[:], AX.X, ALU.add))
            link(dve.tensor_scalar(eid_f[:], eid_f[:], float(E - 1), None, ALU.min))
            dve.tensor_copy(eid[:], eid_f[:, :, 0]).then_inc(route_done, 1)

            for i in range(2):
                dve.wait_ge(sh_split_hi, 2 * i + 2)
                dve.tensor_tensor(flat(gu_lo[i][:]), raw[i][:, 0:C * GU], flat(gu_hi[i][:]).bitcast(F32),
                                  ALU.subtract).then_inc(sh_split_lo, 1)
                dve.tensor_tensor(flat(dn_lo[i][:]), raw[i][:, C * GU:RAW], flat(dn_hi[i][:]).bitcast(F32),
                                  ALU.subtract).then_inc(sh_split_lo, 1)
            dve.wait_ge(mod3_in, 16 * B)
            dve.wait_ge(pad_ready, 3)

            def hid_of(u, pe_steps, act_steps, vec_steps, first):
                if not first:
                    dve.wait_ge(*pe_steps.done(u.back(2).n, "turned"))
                dve.wait_ge(*act_steps.done(u.n, "silu"))
                dve.tensor_tensor(hid[:, u.half, 0:F], PS_U[u.half][:, 0:F], sg_t[:], ALU.mult).then_inc(vec_steps.sem_of["hid"], 1)

            def hidlo(u, act_steps, vec_steps):
                dve.wait_ge(*act_steps.done(u.n, "hid_hi"))
                dve.tensor_tensor(flat(hid_lo[:]), PS_H[:, 0:FK * P], flat(hid_hi[:]).bitcast(F32),
                                  ALU.subtract).then_inc(vec_steps.sem_of["hid_lo"], 1)

            def x_lo(slot, number, act_steps, vec_steps):
                dve.wait_ge(*act_steps.done(number, "hi"))
                dve.tensor_tensor(flat(ex_x_lo[:, slot]), PS_X[:], flat(ex_x_hi[:, slot]).bitcast(F32),
                                  ALU.subtract).then_inc(vec_steps.sem, 1)

            def base_of(t):
                batch = t.n // TPB
                if t.back(2).real():
                    dve.wait_ge(base_out[t.p], 16 * t.half)
                dve.wait_ge(*shu_pe.done(t.unit(1).n, "down"))
                dve.tensor_tensor(base_t[:, t.p, :], PS_Y[:], mod3[:, bass.ds(batch, 1), :].rearrange("p a d -> p (a d)"),
                                  ALU.mult).then_inc(base_vec.sem, 1)
                dve.wait_ge(sr_in[t.p], 16 * t.half + 16)
                dve.wait_ge(*base_vec.done(t.n, "gated"))
                dve.tensor_tensor(base_t[:, t.p, :], base_t[:, t.p, :], xres_t[:, t.p, :], ALU.add).then_inc(base_vec.sem, 1)

            def shared_step(t):
                if t.back(-1).real():
                    x_lo(t.back(-1).p, t.back(-1).n, shx_act, shx_vec)
                for half in range(2):
                    before = t if half else t.back(1)
                    if before.real():
                        hidlo(before.unit(1 - half), shu_act, shu_vec)
                    if t.real():
                        hid_of(t.unit(half), shu_pe, shu_act, shu_vec, not t.back(1).real())
                    if half == 0 and before.real():
                        base_of(before)

            sweep(dve, NT, 1, 1, shared_step)

            wait_shared(dve)
            for p in range(2):
                dve.wait_ge(sc_out[p], 32 * (NT // 2))

            def expert_lo(t, part):
                w_hi, w_lo = (gu_hi, gu_lo) if part == 0 else (dn_hi, dn_lo)
                cols = slice(0, C * GU) if part == 0 else slice(C * GU, RAW)
                dve.wait_ge(*rw_hi_act.done(t.n, "gu_hi" if part == 0 else "dn_hi"))
                dve.tensor_tensor(flat_of(w_lo, t), raw[t.p][:, cols], flat_of(w_hi, t).bitcast(F32),
                                  ALU.subtract).then_inc(rw_lo_vec.sem, 1)

            def y_of_unit(u, t):
                if t.back(1).real():
                    dve.wait_ge(ys_out[u.half], 16 * t.n)
                dve.wait_ge(*ru_pe.done(u.n, "down"))
                dve.tensor_copy(y_rows[:, u.half, :], PS_Y[:]).then_inc(ru_vec.sem_of["y"], 1)

            def routed_step(t):
                for half in range(2):
                    before = t if half else t.back(1)
                    if half and t.back(-1).real():
                        x_lo(0, t.back(-1).unit(0).n, rx_act, rx_vec)
                    if not half and t.real():
                        x_lo(1, t.unit(1).n, rx_act, rx_vec)
                    if before.real():
                        hidlo(before.unit(1 - half), ru_act, ru_vec)
                    if t.real():
                        hid_of(t.unit(half), ru_pe, ru_act, ru_vec, not t.back(1).real())
                    if t.back(-1).real():
                        expert_lo(t.back(-1), half)
                    if before.real():
                        y_of_unit(before.unit(1 - half), before)

            sweep(dve, NJ, 1, 1, routed_step)

            wait_routed(dve)
            dve.wait_ge(gb_in, 16 * B)

            def combine(t):
                batch = t.n // TPB
                dve.wait_ge(y1_in[t.p], 16 * t.half + 16)
                if t.back(2).real():
                    dve.wait_ge(final_out[t.p], 16 * t.half)
                dve.tensor_scalar(cb_out[:, t.p, :], cb_y1[:, t.p, :], w1[:, bass.ds(t.n, 1), :].rearrange("p a b -> p (a b)"),
                                  None, ALU.mult).then_inc(cb_vec.sem, 1)
                dve.wait_ge(y2_in[t.p], 16 * t.half + 16)
                dve.wait_ge(*cb_vec.done(t.n, "first"))
                dve.scalar_tensor_tensor(cb_out[:, t.p, :], cb_y2[:, t.p, :], w2[:, bass.ds(t.n, 1), :].rearrange("p a b -> p (a b)"),
                                         cb_out[:, t.p, :], ALU.mult, ALU.add).then_inc(cb_vec.sem, 1)
                dve.wait_ge(*cb_vec.done(t.n, "both"))
                dve.tensor_tensor(cb_out[:, t.p, :], cb_out[:, t.p, :], cb_gb[:, bass.ds(batch, 1), :].rearrange("p a d -> p (a d)"),
                                  ALU.mult).then_inc(cb_vec.sem, 1)
                dve.wait_ge(cb_in[t.p], 16 * t.half + 16)
                dve.wait_ge(*cb_vec.done(t.n, "gated"))
                dve.tensor_tensor(cb_out[:, t.p, :], cb_out[:, t.p, :], cb_base[:, t.p, :], ALU.add).then_inc(cb_vec.sem, 1)

            sweep(dve, NT, 0, 0, combine)

        @block.tensor
        def _(pe):
            pe.wait_ge(silu_c, 1)
            for m in range(6):
                if m % 2 == 0:
                    pe.wait_ge(wmod_in[m // 2], 16 * C)
                for c in range(C):
                    last = pe.matmul(psum[m][0:B, :], cT[:, c, :], wmod[:, c, m * D:(m + 1) * D], start=(c == 0),
                                     stop=(c == C - 1))
                last.then_inc(mod_mm, 1)
            pe.wait_ge(const_ready, CONSTS)
            pe.wait_ge(mod_vec, MOD_DONE)
            pe.wait_ge(wsplit_lo, NW + 1)

            def t1(t):
                if t.back(1).real():
                    pe.wait_ge(*h1T_act.done(t.back(1).n, "h1T"))
                pe.wait_ge(*hh_vec.done(t.n, "hhat"))
                turn(pe, PS_T1, hh[:, t.p, :]).then_inc(t1_pe.sem, 1)

            def mixed_product(t, m, w, bank):
                return product(pe, bank[:], chunks_of(xm_hi[:, t.p, m]), chunks_of(xm_lo[:, t.p, m]),
                               chunks_of(hi[w]), chunks_of(lo[w]))

            def r(t):
                if t.back(1).real():
                    pe.wait_ge(*sr_act.done(t.back(1).n, "sr"))
                pe.wait_ge(*mix_vec.done(t.n, "mix_lo"))
                mixed_product(t, 0, "r", PS_R).then_inc(rkv_pe.sem, 1)

            def k(t):
                if t.back(1).real():
                    pe.wait_ge(*post_vec.done(t.back(1).n, "z"))
                mixed_product(t, 1, "k", PS_K).then_inc(rkv_pe.sem, 1)

            def v(t):
                if t.back(2).real():
                    pe.wait_ge(*post_vec.done(t.back(2).n, "vk"))
                mixed_product(t, 2, "v", PS_V[t.p]).then_inc(rkv_pe.sem, 1)

            def trw(t):
                if t.back(1).real():
                    pe.wait_ge(*rw_vec.done(t.back(1).n, "rw_lo"))
                pe.wait_ge(*rw_pool.done(t.n, "rw"))
                turn(pe, PS_TR, rw_t).then_inc(rw_pe.sem, 1)

            def o(t):
                if t.back(1).real():
                    pe.wait_ge(*o_act.done(t.back(1).n, "o"))
                pe.wait_ge(*rw_vec.done(t.n, "rw_lo"))
                product(pe, PS_O[:], chunks_of(rw_hi), chunks_of(rw_lo), chunks_of(hi["o"]),
                        chunks_of(lo["o"])).then_inc(rw_pe.sem, 1)

            sweep(pe, NT, *in_turn((r, 0), (trw, 2), (k, 0), (t1, -2), (v, 0), (o, 2)))

            wait_a1(pe)

            def t2(t):
                if t.back(1).real():
                    pe.wait_ge(*h2T_act.done(t.back(1).n, "h2T"))
                pe.wait_ge(*xh2_vec.done(t.n, "xhat"))
                turn(pe, PS_T2, xh2[:, t.p, :]).then_inc(t2_pe.sem, 1)

            def r2(t):
                if t.back(1).real():
                    pe.wait_ge(*post2_act.done(t.back(1).n, "sr2"))
                pe.wait_ge(*mix2_vec.done(t.n, "mix_lo"))
                product(pe, PS_R2[:], chunks_of(xm2_hi[:, t.p, 0]), chunks_of(xm2_lo[:, t.p, 0]), chunks_of(hi["r2"]),
                        chunks_of(lo["r2"])).then_inc(rk2_pe.sem, 1)

            def k2(t):
                if t.back(1).real():
                    pe.wait_ge(*post2_act.done(t.back(1).n, "relu"))
                product(pe, PS_K2[:], chunks_of(xm2_hi[:, t.p, 1]), chunks_of(xm2_lo[:, t.p, 1]), chunks_of(hi["k2"]),
                        chunks_of(lo["k2"])).then_inc(rk2_pe.sem, 1)

            def tk(t):
                if t.back(1).real():
                    pe.wait_ge(*tk_vec.done(t.back(1).n, "k2_lo"))
                pe.wait_ge(*post2_act.done(t.n, "k2"))
                turn(pe, PS_TK, k2_t).then_inc(tk_pe.sem, 1)

            def cv(t):
                if t.back(1).real():
                    pe.wait_ge(*y_vec.done(t.back(1).n, "y"))
                pe.wait_ge(*tk_vec.done(t.n, "k2_lo"))
                product(pe, PS_CV[:], chunks_of(k2_hi), chunks_of(k2_lo), chunks_of(hi["v2"]),
                        chunks_of(lo["v2"])).then_inc(tk_pe.sem, 1)

            def t3(t):
                if t.back(1).real():
                    pe.wait_ge(*t3_vec.done(t.back(1).n, "h3_lo"))
                pe.wait_ge(*ln3_vec.done(t.n, "h3"))
                turn(pe, PS_T3, h3_t[:, t.p, :]).then_inc(t3_pe.sem, 1)

            def router(t):
                if t.back(1).real():
                    pe.wait_ge(*lg_vec.done(t.back(1).n, "copied"))
                pe.wait_ge(*t3_vec.done(t.n, "h3_lo"))
                for c in range(C):
                    pe.matmul(PS_LG[:, 0:16], h3_hi[:, c, :], wrt_hl[:, c, :], start=c == 0, stop=False)
                    last = pe.matmul(PS_LG[:, 0:16], h3_lo[:, c, :], wrt_hl[:, c, :], start=False, stop=c == C - 1)
                last.then_inc(t3_pe.sem, 1)

            sweep(pe, NT, *in_turn((r2, 0), (tk, 1), (t3, 4), (k2, 0), (t2, -2), (router, 4), (cv, 1)))

            wait_a2(pe)

            def route_counts():
                pe.wait_ge(route_vec, ROUTE_BOTH)
                hot = flat(route["both"][:])
                pe.matmul(PS_RT[:, 0:NT * E], earlier[:], hot, start=True, stop=True)
                pe.matmul(PS_RT[:, NT * E:2 * NT * E], ones[:], hot, start=True, stop=True).then_inc(route_pe, 1)

            def up(u, x_slot, w, first, second, pe_steps, act_steps, vec_steps):
                if not first and not second:
                    pe.wait_ge(*vec_steps.done(u.back(2).n, "hid"))
                for bank, col in ((PS_G[u.half], 0), (PS_U[u.half], F)):
                    last = product(pe, bank[:, 0:F], chunks_of(ex_x_hi[:, x_slot]), chunks_of(ex_x_lo[:, x_slot]),
                                   [gu_hi[w][:, c, col:col + F] for c in range(C)],
                                   [gu_lo[w][:, c, col:col + F] for c in range(C)])
                last.then_inc(pe_steps.sem_of["up"], 1)

            def turn_hid(u, first, pe_steps, vec_steps):
                if not first:
                    pe.wait_ge(*vec_steps.done(u.back(1).n, "hid_lo"))
                pe.wait_ge(*vec_steps.done(u.n, "hid"))
                for c in range(FK):
                    last = pe.transpose(PS_H[:, c * P:(c + 1) * P], hid[:, u.half, c * P:(c + 1) * P], ident[:])
                last.then_inc(pe_steps.sem_of["turned"], 1)

            def down(u, w, start, stop, pe_steps, vec_steps):
                pe.wait_ge(*vec_steps.done(u.n, "hid_lo"))
                for c in range(FK):
                    pe.matmul(PS_Y[:], hid_hi[:, c, :], dn_hi[w][:, c, :], start=start and c == 0, stop=False)
                    pe.matmul(PS_Y[:], hid_hi[:, c, :], dn_lo[w][:, c, :], start=False, stop=False)
                    last = pe.matmul(PS_Y[:], hid_lo[:, c, :], dn_hi[w][:, c, :], start=False, stop=stop and c == FK - 1)
                last.then_inc(pe_steps.sem_of["down"], 1)

            def turn_shared(t):
                if t.back(1).real():
                    pe.wait_ge(*shx_vec.done(t.back(1).n, "lo"))
                pe.wait_ge(sx_in[t.p], 16 * t.half + 16)
                turn(pe, PS_X, ex_x[:, t.p, :]).then_inc(shx_pe.sem, 1)

            def shared_step(t):
                if t.back(-1).real():
                    turn_shared(t.back(-1))
                for half in range(2):
                    before = t if half else t.back(1)
                    u = before.unit(1 - half)
                    if before.real():
                        turn_hid(u, not before.back(1).real() and half, shu_pe, shu_vec)
                    if t.real():
                        if half == 0:
                            pe.wait_ge(*shx_vec.done(t.n, "lo"))
                        up(t.unit(half), t.p, half, not t.back(1).real(), False, shu_pe, shu_act, shu_vec)
                    if before.real():
                        if half and before.back(1).real():
                            pe.wait_ge(*base_vec.done(before.back(1).n, "gated"))
                        down(u, 1 - half, half == 1, half == 0, shu_pe, shu_vec)

            route_counts()
            pe.wait_ge(sh_split_lo, 4)
            sweep(pe, NT, 1, 1, shared_step)

            wait_shared(pe)

            def turn_rows(t, half, first):
                u = t.unit(half)
                if not first:
                    pe.wait_ge(*rx_vec.done(u.back(1).n, "lo"))
                pe.wait_ge(ex_in[half], 16 * t.n + 16)
                turn(pe, PS_X, ex_x[:, half, :]).then_inc(rx_pe.sem, 1)

            def routed_step(t):
                for half in range(2):
                    before = t if half else t.back(1)
                    if half and t.back(-1).real():
                        turn_rows(t.back(-1), 0, not t.real())
                    if not half and t.real():
                        turn_rows(t, 1, False)
                    u = before.unit(1 - half)
                    if before.real():
                        turn_hid(u, not before.back(1).real() and half, ru_pe, ru_vec)
                    if t.real():
                        pe.wait_ge(*rx_vec.done(t.unit(half).n, "lo"))
                        if half == 0:
                            pe.wait_ge(*rw_lo_vec.done(t.n, "dn_lo"))
                        up(t.unit(half), half, 2 + t.p, not t.back(1).real(), False, ru_pe, ru_act, ru_vec)
                    if before.real():
                        if half == 0 or before.back(1).real():
                            pe.wait_ge(*ru_vec.done(u.back(1).n, "y"))
                        down(u, 2 + before.p, True, True, ru_pe, ru_vec)

            sweep(pe, NJ, 1, 1, routed_step)



def kernel(**inputs):
    import numpy as np
    import concourse.bacc as bacc
    from concourse.bass_utils import run_bass_kernel_spmd as run

    def a(name):
        return np.asarray(inputs["L0_" + name])

    arrays = {"x": a("attn_x"), "cT": a("c").T, "wmod": a("wmod"), "u": a("attn_tm_u"), "wrT": a("ffn_Wr").T}
    for mine, name in (("ln1_g", "ln1_g"), ("ln1_b", "ln1_b"), ("ln2_g", "ln2_g"), ("ln2_b", "ln2_b"),
                       ("mu_r", "tm_mu_r"), ("mu_k", "tm_mu_k"), ("mu_v", "tm_mu_v"), ("mu_r2", "cm_mu_r"),
                       ("mu_k2", "cm_mu_k")):
        arrays[mine] = a("attn_" + name)
    for mine, name in (("w_r", "tm_Wr"), ("w_k", "tm_Wk"), ("w_v", "tm_Wv"), ("w_o", "tm_Wout"), ("w_r2", "cm_Wr"),
                       ("w_k2", "cm_Wk"), ("w_v2", "cm_Wv")):
        arrays[mine] = a("attn_" + name).T

    def gate_up(gate, up):
        both = np.concatenate([gate.transpose(0, 2, 1), up.transpose(0, 2, 1)], axis=2)
        return both.reshape(-1, C, P, GU).transpose(0, 2, 1, 3).reshape(-1, P, C * GU)

    arrays["sh_gu"] = gate_up(a("ffn_Wsg").reshape(2, F, D), a("ffn_Wsu").reshape(2, F, D))
    arrays["sh_dn"] = a("ffn_Wsd").T.reshape(2, F, D)
    arrays["ex_gu"] = gate_up(a("ffn_Wg"), a("ffn_Wu"))
    arrays["ex_dn"] = a("ffn_Wd").transpose(0, 2, 1)
    arrays = {name: np.ascontiguousarray(v) for name, v in arrays.items()}

    nc = bacc.Bacc("TRN2", target_bir_lowering=False, num_devices=1)
    io = {name: nc.dram_tensor("in_" + name, v.shape, mybir.dt.from_np(v.dtype), kind="ExternalInput").ap()
          for name, v in arrays.items()}
    out = nc.dram_tensor("out", (B, T, D), F32, kind="ExternalOutput").ap()
    build(nc, io, out)
    r = run(nc, [{"in_" + name: v for name, v in arrays.items()}], core_ids=[0])
    return r.results[0]["out"]
```

```python
from contextlib import ExitStack

import concourse.bass as bass
from concourse import mybir

ALU = mybir.AluOpType
ACT = mybir.ActivationFunctionType
AX = mybir.AxisListType
F32 = mybir.dt.float32
F32R = mybir.dt.float32r
I32 = mybir.dt.int32

P = 128
D = 512
C = D // P
B, T = 4, 1024
N = B * T
NT = N // P
TPB = T // P
EPS = 1e-5
E = 8
F = 352
FK = -(-F // P)
GU = 2 * F
RAW = C * GU + FK * D
R = 2 * P
NJ = (2 * N + E * (R - 1)) // R
ZERO_ROWS = NJ * R // NT
ZERO_REPEAT = 3
assert ZERO_ROWS * NT == NJ * R and ZERO_ROWS % ZERO_REPEAT == 0
LN_1E8 = 18.420680743952367


class Steps:

    def __init__(self, sem, *names):
        self.sem = sem
        self.at = {name: i + 1 for i, name in enumerate(names)}

    def done(self, n, name):
        return self.sem, n * len(self.at) + self.at[name]


class Apart:

    def __init__(self, sem, prefix, *names):
        self.sem_of = {name: sem(f"{prefix}_{name}") for name in names}

    def done(self, n, name):
        return self.sem_of[name], n + 1


class Tile:

    def __init__(self, pair, offset, count):
        self.pair, self.offset, self.count = pair, offset, count
        self.p = offset % 2
        self.n = offset if pair is None else 2 * pair + offset
        self.half = offset // 2 if pair is None else pair + offset // 2

    def back(self, d):
        return Tile(self.pair, self.offset - d, self.count)

    def unit(self, half):
        return Unit(2 * self.n + half, half)

    def real(self):
        return self.pair is not None or 0 <= self.offset < self.count


class Unit:
    def __init__(self, n, half):
        self.n, self.half = n, half

    def back(self, d):
        return Unit(self.n - d, (self.half - d) % 2)


def sweep(eng, count, lead, lag, body):
    low = lag + 2 + lag % 2
    high = count - lead - (count - lead) % 2
    for t in range(-lead, low):
        body(Tile(None, t, count))
    with eng.Fori(0, (high - low) // 2) as k:
        for j in range(2):
            body(Tile(k, low + j, count))
    for t in range(high, count + lag):
        body(Tile(None, t, count))


def in_turn(*stages):
    def body(t):
        for stage_of, lag in stages:
            s = t.back(lag)
            if s.real():
                stage_of(s)
    lags = [lag for _, lag in stages]
    return max(0, -min(lags)), max(0, max(lags)), body


def build(nc, io, out):
    x_d = io["x"].rearrange("b t d -> (b t) d")
    out_d = out.rearrange("b t d -> (b t) d")

    def scratch(name, shape, dt=F32):
        return nc.dram_tensor(name, shape, dt).ap()

    mod_d = scratch("mod_rows", [B, 6 * D])
    h_d = scratch("h_rows", [N, D])
    o_d = scratch("timemix_rows", [N, D])
    x2_d = scratch("x2_rows", [N, D])
    xres_d = scratch("xres_rows", [N, D])
    h3_d = scratch("h3_rows", [N, D])
    xs_d = scratch("expert_in_rows", [NJ * R, D])
    ys_d = scratch("expert_out_rows", [NJ * R, D])

    ctx = ExitStack()
    with ctx:
        def sb(name, shape, dt=F32, at=ctx):
            return at.enter_context(nc.sbuf_tensor(name, shape, dt))

        def sem(name):
            return ctx.enter_context(nc.semaphore(name))

        def pair_of_sems(name):
            return [sem(f"{name}{p}") for p in range(2)]

        def steps(name, *names):
            return Steps(sem(name), *names)

        def flat(ap):
            return ap.rearrange("p a b -> p (a b)")

        psum = [ctx.enter_context(nc.psum_tensor(f"bank{i}", [P, D], F32)) for i in range(8)]

        ident = sb("ident", [P, P])
        keep = sb("keep", [P, NT * C])
        keep_i = sb("keep_i", [P, NT * C], I32)
        eps = sb("eps", [P, 1])
        minus_half = sb("minus_half", [P, 1])
        act_col = sb("act_col", [P, 2])
        vecs = sb("vecs", [P, 9, C])
        G1, B1, G2, B2, MUR, MUK, MUV, MUR2, MUK2 = range(9)

        logits = sb("logits", [P, NT, 8])
        wrt = sb("wrt", [P, C, 8])
        wrt_hl = sb("wrt_hl", [P, C, 16], F32R)
        wrt_hi, wrt_lo = wrt_hl[:, :, 0:8], wrt_hl[:, :, 8:16]
        bridge_col = sb("bridge_col", [P, 4])

        W1 = ["r", "k", "v", "o"]
        W2 = ["r2", "k2", "v2"]
        hi, lo = {}, {}
        mixing = ctx.enter_context(ExitStack())
        with ExitStack() as time_mix:
            for w in W1:
                hi[w], lo[w] = sb(f"w_{w}_hi", [P, C, D], F32R, time_mix), sb(f"w_{w}_lo", [P, C, D], F32R, time_mix)

        hin_t = sb("hin_t", [P, 2, D], at=mixing)
        oin_t = sb("oin_t", [P, 2, D], at=mixing)
        x2_t = sb("x2_t", [P, 2, D], at=mixing)
        xh2 = sb("xh2", [P, 2, D], at=mixing)
        diff2 = sb("diff2", [P, C, P], at=mixing)
        mix2 = sb("mix2", [P, 2, C, P], at=mixing)
        xm2_hi = sb("xm2_hi", [P, 2, 2, C, P], F32R, mixing)
        xm2_lo = sb("xm2_lo", [P, 2, 2, C, P], F32R, mixing)
        k2_t = sb("k2_t", [P, D], at=mixing)
        k2_hi = sb("k2_hi", [P, C, P], F32R, mixing)
        k2_lo = sb("k2_lo", [P, C, P], F32R, mixing)
        y_t = sb("y_t", [P, D], at=mixing)
        x2r_t = sb("x2r_t", [P, 2, D], at=mixing)
        xr_t = sb("xr_t", [P, 2, D], at=mixing)
        h3_t = sb("h3_t", [P, 2, D], at=mixing)
        sr2 = sb("sr2", [P, 2, D], at=mixing)
        h3_hi = sb("h3_hi", [P, C, P], F32R, mixing)
        with ExitStack() as first:
            wmod = sb("wmod", [P, C, 6 * D], at=first)
        region2 = mixing.enter_context(ExitStack())
        for w in W2:
            hi[w], lo[w] = sb(f"w_{w}_hi", [P, C, D], F32R, region2), sb(f"w_{w}_lo", [P, C, D], F32R, region2)

        with ExitStack() as a1:
            mod1 = sb("mod1", [P, B, 2, D], at=a1)
            zero_rows = sb("zero_rows", [P, D], at=a1)
            x_t = sb("x_t", [P, 2, D], at=a1)
            st1 = sb("st1", [P, 2, 6], at=a1)
            mv1 = sb("mv1", [P, 2, 2], at=a1)
            rstd1 = sb("rstd1", [P, 2, 1], at=a1)
            st1h = sb("st1h", [P, 2, 6], at=a1)
            mv1h = sb("mv1h", [P, 2, 2], at=a1)
            rstd1h = sb("rstd1h", [P, 2, 1], at=a1)
            var1 = sb("var1", [P, 2], at=a1)
            xh = sb("xh", [P, D], at=a1)
            h_t = sb("h_t", [P, 2, D], at=a1)
            hh = sb("hh", [P, 2, D], at=a1)
            h1T = sb("h1T", [P, 2, C, P + 1], at=a1)
            diff1 = sb("diff1", [P, C, P], at=a1)
            stage = [sb(f"stage{i}", [P, C * D], at=a1) for i in range(2)]
            mix1 = stage[0][:, 0:3 * D].rearrange("p (m c t) -> p m c t", m=3, c=C)
            z_t = stage[1][:, 0:D]
            sk_t = stage[1][:, D:2 * D]
            vk_t = stage[1][:, 2 * D:3 * D]
            rw_t = stage[1][:, 3 * D:4 * D]
            sr_more = sb("sr_more", [P, D], at=a1)
            sr_t = [stage[0][:, 3 * D:4 * D], sr_more[:]]
            xm_hi = sb("xm_hi", [P, 2, 3, C, P], F32R, a1)
            with ExitStack() as early:
                last_stage = sb("last_stage", [P, C * D], at=early)
            xm_lo = sb("xm_lo", [P, 2, 3, C, P], F32R, a1)
            u_bc = sb("u_bc", [P, D], at=a1)
            rw_hi = sb("rw_hi", [P, C, P], F32R, a1)
            rw_lo = sb("rw_lo", [P, C, P], F32R, a1)
            o_t = sb("o_t", [P, 2, D], at=a1)
            cT = sb("cT", [P, C, B], at=a1)
            mod_rows = [ring[0:B, p, :] for ring in (h_t, hh, o_t) for p in range(2)]
            gate_sign, gate_neg = xh[0:B, :], flat(diff1[0:B, :, :])

        with ExitStack() as a2:
            mod2 = sb("mod2", [P, B, 3, D], at=a2)
            st2 = sb("st2", [P, 2, 6], at=a2)
            mv2 = sb("mv2", [P, 2, 2], at=a2)
            var2 = sb("var2", [P, 2], at=a2)
            rstd2 = sb("rstd2", [P, 2, 1], at=a2)
            st3 = sb("st3", [P, 2, 6], at=a2)
            mv3 = sb("mv3", [P, 2, 2], at=a2)
            rstd3 = sb("rstd3", [P, 2, 1], at=a2)
            lg_part = sb("lg_part", [P, 2, 8], at=a2)
            pool_col = sb("pool_col", [P, 1], at=a2)
            h2T = sb("h2T", [P, 2, C, P + 1], at=a2)
            h3_lo = sb("h3_lo", [P, C, P], F32R, a2)

        mixing.close()

        with ExitStack() as at:
            cb_y1 = sb("cb_y1", [P, 2, 2, D], at=at)
            cb_y2 = sb("cb_y2", [P, 2, 2, D], at=at)
            cb_out = sb("cb_out", [P, 2, 2, D], at=at)
        gu_hi = [sb(f"gu{i}_hi", [P, C, GU], F32R) for i in range(2)]
        gu_lo = [sb(f"gu{i}_lo", [P, C, GU], F32R) for i in range(2)]
        dn_hi = [sb(f"dn{i}_hi", [P, FK, D], F32R) for i in range(2)]
        dn_lo = [sb(f"dn{i}_lo", [P, FK, D], F32R) for i in range(2)]
        with ExitStack() as at:
            first_half = sb("first_half", [P, NT // 2, D], at=at)
            route = {name: sb("route_" + name, [P, NT, E], at=at) for name in
                     ("ex", "sc", "oh1", "oh2", "tmp", "both", "cur", "nxt", "pos")}
            row = {name: sb("route_" + name, [P, NT, 1], at=at) for name in ("mx", "sum", "rec", "pick", "s1", "s2")}
            iota_e = sb("iota_e", [P, NT, E], at=at)
            iota_ei = sb("iota_ei", [P, NT, E], I32, at)
            count = {name: sb("route_" + name, [P, 1, E], at=at) for name in ("total", "padded", "end", "end2", "start")}
            count_i = sb("count_i", [P, E], I32, at)
            first_row = sb("first_row", [P, NJ, E], at=at)
            first_row_i = sb("first_row_i", [P, NJ, E], I32, at)
            below = sb("below", [P, NJ, E], at=at)
            eid_f = sb("eid_f", [P, NJ, 1], at=at)
            earlier = sb("earlier", [P, P], at=at)
            ones = sb("ones", [P, P], at=at)
        base = sb("base", [P, NT, D])
        y_rows = sb("y_rows", [P, 2, D])
        sc_t = [y_rows[:, i, :] for i in range(2)]
        gated_t = sb("gated_t", [P, D])
        hid_hi = sb("hid_hi", [P, FK, P], F32R)
        hid_lo = sb("hid_lo", [P, FK, P], F32R)
        w1 = sb("w1", [P, NT, 1])
        w2 = sb("w2", [P, NT, 1])
        slots = sb("slots", [P, 2, NT], I32)
        eid = sb("eid", [P, NJ], I32)
        sg_t = sb("sg_t", [P, F])
        ex_x = sb("ex_x", [P, 2, D])
        ex_x_hi = sb("ex_x_hi", [P, 2, C, P], F32R)
        ex_x_lo = sb("ex_x_lo", [P, 2, C, P], F32R)
        hid = sb("hid", [P, 2, FK * P])
        mod3 = sb("mod3", [P, B, D])
        raw = [sb(f"raw{i}", [P, RAW]) for i in range(2)]

        vec_in = sem("vec_in")
        c_in = sem("c_in")
        wmod_in = [sem(f"wmod_in{q}") for q in range(3)]
        u_in = sem("u_in")
        w_in = [sem(f"w_in{i}") for i in range(3)]
        mod_out = sem("mod_out")
        mod1_in = sem("mod1_in")
        mod2_in = sem("mod2_in")
        x_in = pair_of_sems("x_in")
        h_out = pair_of_sems("h_out")
        o_out = pair_of_sems("o_out")
        h_in = pair_of_sems("h_in")
        o_in = pair_of_sems("o_in")
        x2_out = pair_of_sems("x2_out")
        x2_in = pair_of_sems("x2_in")
        xr_in = pair_of_sems("xr_in")
        xres_out = pair_of_sems("xres_out")
        h3_out = pair_of_sems("h3_out")
        zero_out = sem("zero_out")
        raw_in = pair_of_sems("raw_in")
        mod3_in = sem("mod3_in")
        sx_in = pair_of_sems("sx_in")
        sr_in = pair_of_sems("sr_in")
        sc_in = pair_of_sems("sc_in")
        sc_out = pair_of_sems("sc_out")
        ex_in = pair_of_sems("ex_in")
        ys_out = pair_of_sems("ys_out")
        y1_in = pair_of_sems("y1_in")
        y2_in = pair_of_sems("y2_in")
        final_out = pair_of_sems("final_out")
        const_pool = sem("const_pool")
        const_ready = sem("const_ready")
        silu_c = sem("silu_c")
        mod_mm = sem("mod_mm")
        mod_vec = sem("mod_vec")
        u_ready = sem("u_ready")
        wsplit_hi = sem("wsplit_hi")
        wsplit_lo = sem("wsplit_lo")
        lnx_vec = steps("lnx_vec", "stats", "moments")
        lnx_pool = steps("lnx_pool", "var", "rstd")
        lnh_vec = steps("lnh_vec", "scaled", "h", "stats", "moments")
        lnh_pool = steps("lnh_pool", "var", "rstd")
        hh_vec = steps("hh_vec", "hhat")
        t1_pe = steps("t1_pe", "turned")
        h1T_act = steps("h1T_act", "h1T")
        mix_act = steps("mix_act", "mix_hi")
        mix_vec = steps("mix_vec", "first_col", "mixed", "mix_lo")
        mix_pool = steps("mix_pool", "diff")
        rkv_pe = steps("rkv_pe", "r", "k", "v")
        sr_act = steps("sr_act", "sr")
        sk_act = steps("sk_act", "sk")
        post_vec = steps("post_vec", "z", "vk")
        rw_pool = steps("rw_pool", "rw")
        rw_pe = steps("rw_pe", "turned", "out")
        rw_act = steps("rw_act", "rw_hi")
        rw_vec = steps("rw_vec", "rw_lo")
        o_act = steps("o_act", "o")
        x2_pool = steps("x2_pool", "x2")
        ln2_vec = steps("ln2_vec", "stats", "moments")
        ln2_pool = steps("ln2_pool", "var", "rstd")
        xh2_vec = steps("xh2_vec", "xhat")
        t2_pe = steps("t2_pe", "turned")
        h2T_act = steps("h2T_act", "h2T")
        mix2_act = steps("mix2_act", "mix_hi")
        mix2_vec = steps("mix2_vec", "first_col", "mixed", "mix_lo")
        mix2_pool = steps("mix2_pool", "diff")
        rk2_pe = steps("rk2_pe", "r2", "k2")
        post2_act = steps("post2_act", "sr2", "relu", "k2")
        tk_pe = steps("tk_pe", "turned", "cv")
        tk_act = steps("tk_act", "k2_hi")
        tk_vec = steps("tk_vec", "k2_lo")
        y_vec = steps("y_vec", "y")
        res_pool = steps("res_pool", "x3", "gated", "xres")
        ln3_vec = steps("ln3_vec", "stats", "moments", "scaled", "h3")
        ln3_pool = steps("ln3_pool", "var", "rstd")
        t3_pe = steps("t3_pe", "turned", "logits")
        t3_act = steps("t3_act", "h3_hi")
        t3_vec = steps("t3_vec", "h3_lo")
        lg_vec = steps("lg_vec", "part", "copied")

        zeroed = sem("zeroed")
        ex_const_i = sem("ex_const_i")
        ex_const = sem("ex_const")
        pad_ready = sem("pad_ready")
        route_vec = sem("route_vec")
        route_exp = sem("route_exp")
        route_pe = sem("route_pe")
        route_done = sem("route_done")
        sh_split_hi = sem("sh_split_hi")
        sh_split_lo = sem("sh_split_lo")
        shx_pe = steps("shx_pe", "turned")
        shx_act = steps("shx_act", "hi")
        shx_vec = steps("shx_vec", "lo")
        shu_pe = Apart(sem, "shu_pe", "up", "turned", "down")
        shu_act = steps("shu_act", "silu", "hid_hi")
        shu_vec = Apart(sem, "shu_vec", "hid", "hid_lo")
        base_vec = steps("base_vec", "gated", "base")
        rx_pe = steps("rx_pe", "turned")
        rx_act = steps("rx_act", "hi")
        rx_vec = steps("rx_vec", "lo")
        ru_pe = Apart(sem, "ru_pe", "up", "turned", "down")
        ru_act = steps("ru_act", "silu", "hid_hi")
        ru_vec = Apart(sem, "ru_vec", "hid", "hid_lo", "y")
        rw_hi_act = steps("rw_hi_act", "gu_hi", "dn_hi")
        rw_lo_vec = steps("rw_lo_vec", "gu_lo", "dn_lo")
        cb_act = steps("cb_act", "first")
        cb_vec = steps("cb_vec", "both", "gated", "out")

        ORDER = W1 + W2
        NW = len(ORDER)
        staged = [stage[i % 2][:] for i in range(NW - 1)]
        staged.append(last_stage[:])
        staged_in = [(w_in[i % 2], 16 * (i // 2) + 16) for i in range(NW - 1)] + [(w_in[2], 16)]

        def product(pe, acc, act_hi, act_lo, w_hi, w_lo):
            chunks = len(act_hi)
            for i in range(chunks):
                pe.matmul(acc, act_hi[i], w_hi[i], start=(i == 0), stop=False)
                pe.matmul(acc, act_hi[i], w_lo[i], start=False, stop=False)
                last = pe.matmul(acc, act_lo[i], w_hi[i], start=False, stop=(i == chunks - 1))
            return last

        def chunks_of(ap, n=C):
            return [ap[:, c, :] for c in range(n)]

        def turn(pe, bank, rows):
            for c in range(C):
                last = pe.transpose(bank[:, c * P:(c + 1) * P], rows[:, c * P:(c + 1) * P], ident[:])
            return last

        def bank_chunks(bank):
            return bank[:].rearrange("p (c t) -> p c t", c=C)

        PS_R, PS_K, PS_O, PS_T1, PS_TR = psum[0:5]
        PS_V = psum[5:7]
        PS_R2, PS_K2, PS_CV, PS_T2, PS_TK, PS_T3, PS_LG = psum[0:7]

        def wait_h_rows(eng):
            for p in range(2):
                eng.wait_ge(h_out[p], 16 * (NT // 2))

        def wait_a1(eng):
            for p in range(2):
                eng.wait_ge(h_out[p], 16 * (NT // 2))
                eng.wait_ge(o_out[p], 16 * (NT // 2))

        MOD_AT = [1, 2, 7, 8, 9, 14]
        MOD_DONE = MOD_AT[-1]

        CONSTS = 5
        ROUTE_BOTH = 17


        def bridge(dve, which, reached):
            dve.wait_ge(*reached)
            dve.tensor_copy(bridge_col[:, which:which + 1], eps[:])

        def flat_of(weights, t):
            return flat(weights[t.p][:])

        def scatter(pool, n):
            pool.wait_ge(sc_in[n % 2], 16 * (n // 2) + 16)
            for k in range(2):
                pool.indirect_dma_start(xs_d, bass.IndirectOffsetOnAxis(ap=slots[:, k, n:n + 1], axis=0),
                                        sc_t[n % 2], None).then_inc(sc_out[n % 2], 16)

        def load_raw(sp, i, gu_rows, dn_rows):
            whole = FK - 1
            sp.dma_start(raw[i][:, 0:C * GU], gu_rows).then_inc(raw_in[i], 16)
            sp.dma_start(raw[i][:, C * GU:C * GU + whole * D].rearrange("p (k d) -> p k d", k=whole),
                         dn_rows[0:whole * P, :].rearrange("(k p) d -> p k d", p=P)).then_inc(raw_in[i], 16)
            sp.dma_start(raw[i][0:F - whole * P, C * GU + whole * D:RAW], dn_rows[whole * P:F, :]).then_inc(raw_in[i], 16)

        def wait_a2(eng):
            eng.wait_ge(*lg_vec.done(NT - 1, "copied"))
            for p in range(2):
                eng.wait_ge(xres_out[p], 16 * (NT // 2))
                eng.wait_ge(h3_out[p], 16 * (NT // 2))

        LAST = Tile(None, NT - 1, NT)
        LAST_UNIT = LAST.unit(1)
        FIRST = Tile(None, 0, NJ)

        def wait_routed(eng):
            for p in range(2):
                eng.wait_ge(ys_out[p], 16 * NJ)

        PS_X, PS_G, PS_U, PS_H, PS_RT, PS_Y = psum[0], psum[1:3], psum[3:5], psum[5], psum[6], psum[7]
        PS_PRE = PS_RT[:, 0:NT * E].rearrange("p (t e) -> p t e", e=E)
        PS_TOT = PS_RT[:, NT * E:2 * NT * E].rearrange("p (t e) -> p t e", e=E)

        block = ctx.enter_context(nc.Block())

        @block.sync
        def _(sp):
            names = ["ln1_g", "ln1_b", "ln2_g", "ln2_b", "mu_r", "mu_k", "mu_v", "mu_r2", "mu_k2"]

            def load_wmod(q):
                for c in range(C):
                    sp.dma_start(wmod[:, c, 2 * q * D:2 * (q + 1) * D],
                                 io["wmod"][c * P:(c + 1) * P, 2 * q * D:2 * (q + 1) * D]).then_inc(wmod_in[q], 16)

            def load_weight(i):
                if 2 <= i < NW - 1:
                    sp.wait_ge(wsplit_lo, i - 1)
                sp.dma_start(staged[i].rearrange("p (c n) -> p c n", c=C),
                             io["w_" + ORDER[i]].rearrange("(c p) n -> p c n", p=P)).then_inc(staged_in[i][0], 16)

            def store_mod(m):
                sp.wait_ge(mod_vec, MOD_AT[m])
                sp.dma_start(mod_d[:, m * D:(m + 1) * D], mod_rows[m]).then_inc(mod_out, 16)

            sp.dma_start(cT[:], io["cT"].rearrange("(c p) b -> p c b", p=P)).then_inc(c_in, 16)
            load_wmod(0)
            load_weight(0)
            load_weight(1)
            load_wmod(1)
            load_wmod(2)
            for t in range(2):
                sp.dma_start(x_t[:, t, :], x_d[t * P:(t + 1) * P, :]).then_inc(x_in[t], 16)
            store_mod(0)
            store_mod(1)
            for i in range(2, len(W1)):
                load_weight(i)
            sp.wait_ge(mod_out, 32)
            for b in range(B):
                sp.dma_start(flat(mod1[:, b]), mod_d[b, 0:2 * D].partition_broadcast(P)).then_inc(mod1_in, 16)
            for m in range(2, 6):
                store_mod(m)
            for i in range(len(W1), NW - 1):
                load_weight(i)
            sp.wait_ge(*lnh_vec.done(0, "scaled"))
            sp.dma_start(x_t[:, 0, :], x_d[2 * P:3 * P, :]).then_inc(x_in[0], 16)
            sp.dma_start(u_bc[:], io["u"].partition_broadcast(P)).then_inc(u_in, 16)
            sp.dma_start(wrt[:], io["wrT"].rearrange("(c p) e -> p c e", p=P)).then_inc(vec_in, 16)
            for i, name in enumerate(names):
                sp.dma_start(vecs[:, i, :], io[name].rearrange("(c p) -> p c", p=P),
                             allow_slow_non_contiguous=True).then_inc(vec_in, 16)
            load_weight(NW - 1)
            sp.wait_ge(mod_out, 96)

            def load_x(t):
                if t.pair is None and t.n < 3:
                    return
                row = sp.snap(t.n * P) if t.pair is not None else t.n * P
                if t.back(2).real():
                    sp.wait_ge(*lnh_vec.done(t.back(2).n, "scaled"))
                sp.dma_start(x_t[:, t.p, :], x_d[bass.ds(row, P), :]).then_inc(x_in[t.p], 16)

            def store_h(t):
                row = sp.snap(t.n * P) if t.pair is not None else t.n * P
                sp.wait_ge(*lnh_vec.done(t.n, "h"))
                sp.dma_start(h_d[bass.ds(row, P), :], h_t[:, t.p, :]).then_inc(h_out[t.p], 16)

            def store_o(t):
                row = sp.snap(t.n * P) if t.pair is not None else t.n * P
                sp.wait_ge(*o_act.done(t.n, "o"))
                sp.dma_start(o_d[bass.ds(row, P), :], o_t[:, t.p, :]).then_inc(o_out[t.p], 16)

            def zero_part(t):
                row = sp.snap(t.n * ZERO_ROWS) if t.pair is not None else t.n * ZERO_ROWS
                sp.dma_start(xs_d[bass.ds(row, ZERO_ROWS), :].rearrange("(p r) d -> p r d", r=ZERO_REPEAT),
                             zero_rows[0:ZERO_ROWS // ZERO_REPEAT, :].unsqueeze(1).to_broadcast(
                                 [ZERO_ROWS // ZERO_REPEAT, ZERO_REPEAT, D])).then_inc(zero_out, 16)

            sp.wait_ge(zeroed, 1)
            def load_ho(t):
                row = sp.snap(t.n * P) if t.pair is not None else t.n * P
                if t.back(2).real():
                    sp.wait_ge(*x2_pool.done(t.back(2).n, "x2"))
                sp.dma_start(hin_t[:, t.p, :], h_d[bass.ds(row, P), :]).then_inc(h_in[t.p], 16)
                sp.dma_start(oin_t[:, t.p, :], o_d[bass.ds(row, P), :]).then_inc(o_in[t.p], 16)

            def first_ho(t):
                if t.pair is None and t.n == NT - 1:
                    sp.wait_ge(*rkv_pe.done(t.n, "v"))
                    for p in range(2):
                        sp.wait_ge(h_out[p], 16 * (NT // 2))
                        sp.wait_ge(o_out[p], 16 * (NT // 2 - 1))
                        load_ho(Tile(None, p, NT))

            def store_x2(t):
                row = sp.snap(t.n * P) if t.pair is not None else t.n * P
                sp.wait_ge(*x2_pool.done(t.n, "x2"))
                sp.dma_start(x2_d[bass.ds(row, P), :], x2_t[:, t.p, :]).then_inc(x2_out[t.p], 16)

            def next_ho(t):
                if t.pair is None and t.n >= NT - 2:
                    store_x2(Tile(None, t.n - (NT - 2), NT))
                    load_ho(Tile(None, t.n - (NT - 4), NT))

            sweep(sp, NT, *in_turn((store_o, 3), (load_x, -5), (store_h, -3), (zero_part, 0), (first_ho, 1), (next_ho, 3)))

            wait_a1(sp)
            sp.wait_ge(zero_out, 16 * NT)
            def later_ho(t):
                if t.pair is not None or t.n >= 4:
                    load_ho(t)

            def later_x2(t):
                if t.pair is not None or t.n >= 2:
                    store_x2(t)

            def load_x2(t):
                row = sp.snap(t.n * P) if t.pair is not None else t.n * P
                if t.back(2).real():
                    sp.wait_ge(*res_pool.done(t.back(2).n, "x3"))
                sp.wait_ge(x2_out[t.p], 16 * t.half + 16)
                sp.dma_start(x2r_t[:, t.p, :], x2_d[bass.ds(row, P), :]).then_inc(x2_in[t.p], 16)

            def load_xr(t):
                row = sp.snap(t.n * P) if t.pair is not None else t.n * P
                if t.back(2).real():
                    sp.wait_ge(*ln3_vec.done(t.back(2).n, "scaled"))
                    sp.wait_ge(xres_out[t.p], 16 * t.half)
                sp.dma_start(xr_t[:, t.p, :], x_d[bass.ds(row, P), :]).then_inc(xr_in[t.p], 16)

            def store_xres(t):
                row = sp.snap(t.n * P) if t.pair is not None else t.n * P
                sp.wait_ge(*res_pool.done(t.n, "xres"))
                sp.dma_start(xres_d[bass.ds(row, P), :], xr_t[:, t.p, :]).then_inc(xres_out[t.p], 16)

            def store_h3(t):
                row = sp.snap(t.n * P) if t.pair is not None else t.n * P
                sp.wait_ge(*ln3_vec.done(t.n, "h3"))
                sp.dma_start(h3_d[bass.ds(row, P), :], h3_t[:, t.p, :]).then_inc(h3_out[t.p], 16)

            def load_mod2(t):
                if t.pair is None and t.n == 0:
                    for b in range(B):
                        sp.dma_start(flat(mod2[:, b]), mod_d[b, 2 * D:5 * D].partition_broadcast(P)).then_inc(mod2_in, 16)

            def load_rows_of(t):
                row_of = sp.snap(t.n * P) if t.pair is not None else t.n * P
                if t.back(2).real():
                    sp.wait_ge(*shx_pe.done(t.back(2).n, "turned"))
                sp.dma_start(ex_x[:, t.p, :], h3_d[bass.ds(row_of, P), :]).then_inc(sx_in[t.p], 16)

            def load_ahead(t):
                if t.pair is None and t.n < 2:
                    sp.wait_ge(pad_ready, 2)
                    load_raw(sp, t.n, io["sh_gu"][t.n], io["sh_dn"][t.n])
                if t.pair is None and t.n == 2:
                    for b in range(B):
                        sp.dma_start(mod3[:, b, :], mod_d[b, 5 * D:6 * D].partition_broadcast(P)).then_inc(mod3_in, 16)
                if t.pair is None and t.n == NT - 1:
                    for p in range(2):
                        sp.wait_ge(h3_out[p], 16)
                        load_rows_of(Tile(None, p, NT))

            sweep(sp, NT, *in_turn((later_ho, -5), (load_mod2, 0), (load_ahead, 1), (load_x2, 1), (store_xres, 2), (load_xr, 1), (store_h3, 3), (later_x2, -4)))

            wait_a2(sp)

            def load_residual(t):
                row_of = sp.snap(t.n * P) if t.pair is not None else t.n * P
                sp.dma_start(base[:, bass.ds(t.n, 1), :].rearrange("p a d -> p (a d)"),
                             xres_d[bass.ds(row_of, P), :]).then_inc(sr_in[t.p], 16)

            def load_expert(t):
                e = sp.value_load(eid[0:1, bass.ds(t.n, 1)], min_val=0, max_val=E - 1)
                if t.back(2).real():
                    sp.wait_ge(*rw_lo_vec.done(t.back(2).n, "dn_lo"))
                else:
                    sp.wait_ge(sh_split_lo, 4)
                load_raw(sp, t.p, io["ex_gu"][bass.ds(e, 1)].rearrange("a p c -> (a p) c"),
                         io["ex_dn"][bass.ds(e, 1)].rearrange("a f d -> (a f) d"))

            def shared_step(t):
                if t.back(-2).real():
                    if t.pair is not None or t.n >= 0:
                        load_rows_of(t.back(-2))
                    load_residual(t.back(-2))
                if t.pair is None and t.n == 3:
                    sp.wait_ge(route_done, 1)
                    for first in range(2):
                        load_expert(Tile(None, first, NJ))

            sweep(sp, NT, 2, 2, shared_step)

            def load_rows(t):
                for half in range(2):
                    u = t.unit(half)
                    row_of = sp.snap(u.n * P) if t.pair is not None else u.n * P
                    if t.back(1).real():
                        sp.wait_ge(*rx_pe.done(u.back(2).n, "turned"))
                    else:
                        sp.wait_ge(*shx_pe.done(NT - 2 + half, "turned"))
                    sp.dma_start(ex_x[:, half, :], xs_d[bass.ds(row_of, P), :]).then_inc(ex_in[half], 16)

            for p in range(2):
                sp.wait_ge(sc_out[p], 32 * (NT // 2))

            def routed_step(t):
                if t.back(-1).real():
                    load_rows(t.back(-1))
                if t.real() and t.back(-2).real():
                    load_expert(t.back(-2))

            sweep(sp, NJ, 2, 0, routed_step)

            def store_out(t):
                row_of = sp.snap(t.n * 2 * P) if t.pair is not None else t.n * 2 * P
                sp.wait_ge(*cb_vec.done(t.n, "out"))
                sp.dma_start(out_d[bass.ds(row_of, 2 * P), :].rearrange("(a p) d -> p a d", p=P),
                             cb_out[:, t.p]).then_inc(final_out[t.p], 16)

            sweep(sp, NT // 2, *in_turn((store_out, 0)))
            for p in range(2):
                sp.wait_ge(final_out[p], 16 * (NT // 4))
            sp.wait_ge(zero_out, 16 * NT)

        @block.gpsimd
        def _(pool):
            pool.memset(ident[:], 0.0).then_inc(const_pool, 1)
            pool.iota(keep_i[:].rearrange("p (t c) -> p t c", c=C), [[0, NT // TPB], [1, TPB], [0, C]], base=0,
                      channel_multiplier=0).then_inc(const_pool, 1)
            pool.memset(zero_rows[:], 0.0).then_inc(zeroed, 1)
            pool.memset(eps[:], EPS).then_inc(const_ready, 1)
            pool.memset(minus_half[:], -0.5).then_inc(const_ready, 1)
            pool.memset(h1T[:, 1, :, P:P + 1], 0.0).then_inc(const_ready, 1)
            pool.wait_ge(const_pool, 2)
            pool.affine_select(out=ident[:], in_=ident[:], compare_op=ALU.not_equal, fill=1.0, base=0,
                               pattern=[[-1, P]], channel_multiplier=1).then_inc(const_ready, 1)
            pool.tensor_scalar(keep[:], keep_i[:], 0.0, None, ALU.is_gt).then_inc(const_ready, 1)
            pool.wait_ge(const_ready, CONSTS)

            def x_rstd(t):
                pool.wait_ge(*lnx_vec.done(t.n, "moments"))
                pool.tensor_tensor(var1[:, 0:1], mv1[:, t.p, 1:2], eps[:], ALU.add).then_inc(lnx_pool.sem, 1)
                pool.wait_ge(*lnx_pool.done(t.n, "var"))
                pool.tensor_tensor(rstd1[:, t.p, :], var1[:, 0:1], minus_half[:], ALU.pow).then_inc(lnx_pool.sem, 1)

            def h_rstd(t):
                pool.wait_ge(*lnh_vec.done(t.n, "moments"))
                pool.tensor_tensor(var1[:, 1:2], mv1h[:, t.p, 1:2], eps[:], ALU.add).then_inc(lnh_pool.sem, 1)
                pool.wait_ge(*lnh_pool.done(t.n, "var"))
                pool.tensor_tensor(rstd1h[:, t.p, :], var1[:, 1:2], minus_half[:], ALU.pow).then_inc(lnh_pool.sem, 1)

            def diff(t):
                pool.wait_ge(*h1T_act.done(t.n, "h1T"))
                pool.wait_ge(*mix_vec.done(t.n, "first_col"))
                pool.tensor_tensor(diff1[:], h1T[:, t.p, :, 1:P + 1], h1T[:, t.p, :, 0:P],
                                   ALU.subtract).then_inc(mix_pool.sem, 1)

            def rw(t):
                pool.wait_ge(*sr_act.done(t.n, "sr"))
                pool.wait_ge(*post_vec.done(t.n, "vk"))
                if t.back(1).real():
                    pool.wait_ge(*rw_pe.done(t.back(1).n, "turned"))
                pool.tensor_tensor(rw_t, vk_t, sr_t[t.p], ALU.mult).then_inc(rw_pool.sem, 1)

            sweep(pool, NT, *in_turn((diff, -1), (x_rstd, -4), (rw, 1), (h_rstd, -3)))

            wait_h_rows(pool)
            pool.memset(h2T[:, 1, :, P:P + 1], 0.0).then_inc(const_ready, 1)

            def x2(t):
                if t.back(2).real():
                    pool.wait_ge(*xh2_vec.done(t.back(2).n, "xhat"))
                    pool.wait_ge(x2_out[t.p], 16 * t.half)
                pool.wait_ge(h_in[t.p], 16 * t.half + 16)
                pool.wait_ge(o_in[t.p], 16 * t.half + 16)
                pool.tensor_tensor(x2_t[:, t.p, :], hin_t[:, t.p, :], oin_t[:, t.p, :], ALU.add).then_inc(x2_pool.sem, 1)

            def rstd_2(t):
                pool.wait_ge(*ln2_vec.done(t.n, "moments"))
                pool.tensor_tensor(var2[:, 0:1], mv2[:, t.p, 1:2], eps[:], ALU.add).then_inc(ln2_pool.sem, 1)
                pool.wait_ge(*ln2_pool.done(t.n, "var"))
                pool.tensor_tensor(rstd2[:, t.p, :], var2[:, 0:1], minus_half[:], ALU.pow).then_inc(ln2_pool.sem, 1)

            def diff_2(t):
                pool.wait_ge(*h2T_act.done(t.n, "h2T"))
                pool.wait_ge(*mix2_vec.done(t.n, "first_col"))
                pool.tensor_tensor(diff2[:], h2T[:, t.p, :, 1:P + 1], h2T[:, t.p, :, 0:P],
                                   ALU.subtract).then_inc(mix2_pool.sem, 1)

            def x3(t):
                pool.wait_ge(x2_in[t.p], 16 * t.half + 16)
                pool.wait_ge(*y_vec.done(t.n, "y"))
                pool.tensor_tensor(y_t[:], y_t[:], x2r_t[:, t.p, :], ALU.add).then_inc(res_pool.sem, 1)

            def gated(t):
                batch = t.n // TPB
                if t.pair is None and t.n == 0:
                    pool.wait_ge(mod2_in, 16 * B)
                pool.wait_ge(*res_pool.done(t.n, "x3"))
                pool.tensor_tensor(pool_col[:], eps[:], eps[:], ALU.add)
                pool.tensor_tensor(y_t[:], y_t[:], mod2[:, bass.ds(batch, 1), 0, :].rearrange("p a d -> p (a d)"),
                                   ALU.mult).then_inc(res_pool.sem, 1)

            def xres(t):
                pool.wait_ge(xr_in[t.p], 16 * t.half + 16)
                pool.wait_ge(*res_pool.done(t.n, "gated"))
                pool.tensor_tensor(xr_t[:, t.p, :], xr_t[:, t.p, :], y_t[:], ALU.add).then_inc(res_pool.sem, 1)

            def rstd_3(t):
                pool.wait_ge(*ln3_vec.done(t.n, "moments"))
                pool.tensor_tensor(var2[:, 1:2], mv3[:, t.p, 1:2], eps[:], ALU.add).then_inc(ln3_pool.sem, 1)
                pool.wait_ge(*ln3_pool.done(t.n, "var"))
                pool.tensor_tensor(rstd3[:, t.p, :], var2[:, 1:2], minus_half[:], ALU.pow).then_inc(ln3_pool.sem, 1)

            sweep(pool, NT, *in_turn((diff_2, -1), (x3, 2), (rstd_3, 3), (rstd_2, -3), (gated, 2), (xres, 2), (x2, -4)))

            wait_a2(pool)
            pool.iota(iota_ei[:], [[0, NT], [1, E]], base=-E, channel_multiplier=0).then_inc(ex_const_i, 1)
            pool.iota(first_row_i[:], [[R, NJ], [0, E]], base=0, channel_multiplier=0).then_inc(ex_const_i, 1)
            pool.memset(ones[:], 1.0).then_inc(ex_const_i, 1)
            pool.wait_ge(ex_const_i, 3)
            pool.tensor_copy(iota_e[:], iota_ei[:]).then_inc(ex_const, 1)
            pool.tensor_copy(first_row[:], first_row_i[:]).then_inc(ex_const, 1)
            pool.affine_select(out=earlier[:], in_=ones[:], compare_op=ALU.is_gt, fill=0.0, base=0,
                               pattern=[[1, P]], channel_multiplier=-1).then_inc(ex_const, 1)

            pool.wait_ge(route_done, 1)
            pool.wait_ge(zero_out, 16 * NT)
            for n in range(NT):
                if n >= 2:
                    pool.wait_ge(sc_out[n % 2], 32 * (n // 2))
                pool.dma_start(sc_t[n % 2], h3_d[n * P:(n + 1) * P, :]).then_inc(sc_in[n % 2], 16)
                if n >= 1:
                    scatter(pool, n - 1)
            scatter(pool, NT - 1)

            wait_routed(pool)
            for pair in range(NT // 2):
                for k, (rows, arrived) in enumerate(((cb_y1, y1_in), (cb_y2, y2_in))):
                    if pair >= 2:
                        pool.wait_ge(*(cb_vec.done(pair - 2, "both") if k else cb_act.done(pair - 2, "first")))
                    for a in range(2):
                        n = 2 * pair + a
                        pool.indirect_dma_start(rows[:, pair % 2, a, :], None, ys_d,
                                                bass.IndirectOffsetOnAxis(ap=slots[:, k, n:n + 1], axis=0)
                                                ).then_inc(arrived[pair % 2], 16)

        @block.scalar
        def _(act):
            act.wait_ge(c_in, 16)
            act.activation(cT[:], cT[:], ACT.Silu).then_inc(silu_c, 1)
            for i, w in enumerate(ORDER):
                act.wait_ge(*staged_in[i])
                if w == W2[0]:
                    act.wait_ge(mod_mm, 6)
                act.activation(flat(hi[w][:]), staged[i], ACT.Copy).then_inc(wsplit_hi, 1)
            act.wait_ge(vec_in, 160)
            act.activation(wrt_hi, wrt[:], ACT.Copy).then_inc(wsplit_hi, 1)

            def h1T_of(t):
                act.wait_ge(*t1_pe.done(t.n, "turned"))
                if t.back(1).real():
                    act.wait_ge(*mix_vec.done(t.back(1).n, "first_col"))
                for c in range(C):
                    last = act.activation(h1T[:, t.p, c, 1:P + 1], PS_T1[:, c * P:(c + 1) * P], ACT.Identity,
                                          bias=vecs[:, B1, c:c + 1], scale=vecs[:, G1, c:c + 1])
                last.then_inc(h1T_act.sem, 1)

            def mix_hi(t):
                if t.back(2).real():
                    act.wait_ge(*rkv_pe.done(t.back(2).n, "v"))
                act.wait_ge(*mix_vec.done(t.n, "mixed"))
                act.activation(xm_hi[:, t.p].rearrange("p m c t -> p (m c t)"), stage[0][:, 0:3 * D],
                               ACT.Copy).then_inc(mix_act.sem, 1)

            def sr(t):
                if t.back(2).real():
                    act.wait_ge(*rw_pool.done(t.back(2).n, "rw"))
                act.wait_ge(*rkv_pe.done(t.n, "r"))
                act.activation(sr_t[t.p], PS_R[:], ACT.Sigmoid).then_inc(sr_act.sem, 1)

            def sk(t):
                act.wait_ge(*post_vec.done(t.n, "z"))
                act.activation(sk_t, z_t, ACT.Sigmoid).then_inc(sk_act.sem, 1)

            def rwhi(t):
                if t.back(1).real():
                    act.wait_ge(*rw_pe.done(t.back(1).n, "out"))
                act.wait_ge(*rw_pe.done(t.n, "turned"))
                act.activation(flat(rw_hi[:]), PS_TR[:], ACT.Copy).then_inc(rw_act.sem, 1)

            def o_rows(t):
                if t.back(2).real():
                    act.wait_ge(o_out[t.p], 16 * t.half)
                act.wait_ge(*rw_pe.done(t.n, "out"))
                act.activation(o_t[:, t.p, :], PS_O[:], ACT.Copy).then_inc(o_act.sem, 1)

            sweep(act, NT, *in_turn((o_rows, 3), (sk, 1), (sr, 0), (rwhi, 2), (mix_hi, -1), (h1T_of, -2)))

            wait_h_rows(act)

            def h2T_of(t):
                act.wait_ge(*t2_pe.done(t.n, "turned"))
                if t.back(1).real():
                    act.wait_ge(*mix2_vec.done(t.back(1).n, "first_col"))
                for c in range(C):
                    last = act.activation(h2T[:, t.p, c, 1:P + 1], PS_T2[:, c * P:(c + 1) * P], ACT.Identity,
                                          bias=vecs[:, B2, c:c + 1], scale=vecs[:, G2, c:c + 1])
                last.then_inc(h2T_act.sem, 1)

            def mix2_hi(t):
                if t.back(2).real():
                    act.wait_ge(*rk2_pe.done(t.back(2).n, "k2"))
                act.wait_ge(*mix2_vec.done(t.n, "mixed"))
                act.activation(xm2_hi[:, t.p].rearrange("p m c t -> p (m c t)"), mix2[:].rearrange("p m c t -> p (m c t)"),
                               ACT.Copy).then_inc(mix2_act.sem, 1)

            def sr2_of(t):
                if t.back(2).real():
                    act.wait_ge(*y_vec.done(t.back(2).n, "y"))
                act.wait_ge(*rk2_pe.done(t.n, "r2"))
                act.activation(sr2[:, t.p, :], PS_R2[:], ACT.Sigmoid).then_inc(post2_act.sem, 1)

            def k2_of(t):
                if t.back(1).real():
                    act.wait_ge(*tk_pe.done(t.back(1).n, "turned"))
                act.wait_ge(*rk2_pe.done(t.n, "k2"))
                act.activation(k2_t[:], PS_K2[:], ACT.Relu).then_inc(post2_act.sem, 1)
                act.wait_ge(*post2_act.done(t.n, "relu"))
                act.activation(k2_t[:], k2_t[:], ACT.Square).then_inc(post2_act.sem, 1)

            def k2hi(t):
                if t.back(1).real():
                    act.wait_ge(*tk_pe.done(t.back(1).n, "cv"))
                act.wait_ge(*tk_pe.done(t.n, "turned"))
                act.activation(flat(k2_hi[:]), PS_TK[:], ACT.Copy).then_inc(tk_act.sem, 1)

            def h3hi(t):
                if t.back(1).real():
                    act.wait_ge(*t3_pe.done(t.back(1).n, "logits"))
                act.wait_ge(*t3_pe.done(t.n, "turned"))
                act.activation(flat(h3_hi[:]), PS_T3[:], ACT.Copy).then_inc(t3_act.sem, 1)

            def shared_x_hi(t):
                if t.back(2).real():
                    act.wait_ge(*shu_pe.done(t.back(2).unit(1).n, "up"))
                act.wait_ge(*shx_pe.done(t.n, "turned"))
                act.activation(flat(ex_x_hi[:, t.p]), PS_X[:], ACT.Copy).then_inc(shx_act.sem, 1)

            def gu_hi_of(i):
                act.wait_ge(raw_in[i], 48)
                act.activation(flat(gu_hi[i][:]), raw[i][:, 0:C * GU], ACT.Copy).then_inc(sh_split_hi, 1)

            def first_gu0(t):
                if t.pair is None and t.n == NT - 1:
                    act.wait_ge(*xh2_vec.done(t.n, "xhat"))
                    for p in range(2):
                        act.wait_ge(x2_out[p], 16 * (NT // 2))
                    gu_hi_of(0)

            def first_gu1(t):
                if t.pair is None and t.n == NT - 1:
                    act.wait_ge(*t2_pe.done(t.n, "turned"))
                    act.wait_ge(*mix2_vec.done(t.n, "mix_lo"))
                    act.wait_ge(*rk2_pe.done(t.n, "k2"))
                    gu_hi_of(1)

            def first_shared(t):
                if t.pair is None and t.n == NT - 1:
                    shared_x_hi(Tile(None, 0, NT))

            sweep(act, NT, *in_turn((sr2_of, 0), (k2hi, 1), (h3hi, 4), (mix2_hi, -1), (k2_of, 0), (h2T_of, -2),
                                    (first_gu0, 1), (first_gu1, 2), (first_shared, 4)))

            wait_a2(act)
            for i in range(2):
                act.activation(flat(dn_hi[i][:]), raw[i][:, C * GU:RAW], ACT.Copy).then_inc(sh_split_hi, 1)

            def hidhi(u, first, pe_steps, act_steps):
                if not first:
                    act.wait_ge(*pe_steps.done(u.back(1).n, "down"))
                elif pe_steps is ru_pe:
                    act.wait_ge(*shu_pe.done(LAST_UNIT.n, "down"))
                act.wait_ge(*pe_steps.done(u.n, "turned"))
                act.activation(flat(hid_hi[:]), PS_H[:, 0:FK * P], ACT.Copy).then_inc(act_steps.sem, 1)

            def silu(u, first, pe_steps, act_steps, vec_steps):
                if not first:
                    act.wait_ge(*vec_steps.done(u.back(1).n, "hid"))
                elif pe_steps is ru_pe:
                    act.wait_ge(*shu_vec.done(LAST_UNIT.n, "hid"))
                act.wait_ge(*pe_steps.done(u.n, "up"))
                act.activation(sg_t[:], PS_G[u.half][:, 0:F], ACT.Silu).then_inc(act_steps.sem, 1)

            def routed_x_hi(u, first):
                if not first:
                    act.wait_ge(*ru_pe.done(u.back(2).n, "up"))
                else:
                    act.wait_ge(*shu_pe.done(Tile(None, NT - 2 + u.half, NT).unit(1).n, "up"))
                act.wait_ge(*rx_pe.done(u.n, "turned"))
                act.activation(flat(ex_x_hi[:, u.half]), PS_X[:], ACT.Copy).then_inc(rx_act.sem, 1)

            def expert_hi(t, part):
                if t.back(2).real():
                    users, last = ru_pe, t.back(2).unit(1).n
                else:
                    users, last = shu_pe, LAST.unit(t.p).n
                if part == 0:
                    act.wait_ge(*users.done(last, "up"))
                    act.wait_ge(raw_in[t.p], 48 * t.half + 96)
                    act.activation(flat_of(gu_hi, t), raw[t.p][:, 0:C * GU], ACT.Copy).then_inc(rw_hi_act.sem, 1)
                else:
                    act.wait_ge(*users.done(last, "down"))
                    act.activation(flat_of(dn_hi, t), raw[t.p][:, C * GU:RAW], ACT.Copy).then_inc(rw_hi_act.sem, 1)

            def shared_step(t):
                if t.real() and t.back(-1).real():
                    shared_x_hi(t.back(-1))
                for half in range(2):
                    before = t if half else t.back(1)
                    if before.real():
                        u = before.unit(1 - half)
                        hidhi(u, not before.back(1).real() and half, shu_pe, shu_act)
                    if t.pair is None and t.n == NT - 1 and half:
                        expert_hi(FIRST, 0)
                    if t.real():
                        silu(t.unit(half), not t.back(1).real() and not half, shu_pe, shu_act, shu_vec)
                if t.pair is None and t.n == NT - 1:
                    routed_x_hi(FIRST.unit(0), True)
                if t.pair is None and t.n == -1:
                    act.wait_ge(route_vec, 2)
                    act.activation(route["ex"][:], route["ex"][:], ACT.Exp).then_inc(route_exp, 1)

            sweep(act, NT, 1, 1, shared_step)

            def store_y(t, half):
                u = t.unit(half)
                row_of = act.snap(u.n * P) if t.pair is not None else u.n * P
                act.wait_ge(*ru_vec.done(u.n, "y"))
                act.dma_start(ys_d[bass.ds(row_of, P), :], y_rows[:, half, :]).then_inc(ys_out[half], 16)

            def routed_step(t):
                for half in range(2):
                    before = t if half else t.back(1)
                    after = t.back(-1) if half else t
                    if t.back(-1).real() and not (t.pair is None and t.n == -1 and half == 0):
                        expert_hi(t.back(-1), half)
                    if half and t.back(-1).real() and t.real():
                        routed_x_hi(t.back(-1).unit(0), False)
                    if not half and t.real():
                        routed_x_hi(t.unit(1), not t.back(1).real())
                    if before.real():
                        hidhi(before.unit(1 - half), not before.back(1).real() and half, ru_pe, ru_act)
                    if t.real():
                        silu(t.unit(half), not t.back(1).real() and not half, ru_pe, ru_act, ru_vec)
                    if t.back(1).real():
                        store_y(t.back(1), half)

            sweep(act, NJ, 1, 1, routed_step)

            wait_routed(act)

            def first_product(t):
                if t.back(2).real():
                    act.wait_ge(final_out[t.p], 16 * t.half)
                act.wait_ge(y1_in[t.p], 32 * t.half + 32)
                act.activation(act_col[:, t.p:t.p + 1], eps[:], ACT.Copy)
                for a in range(2):
                    last = act.activation(cb_out[:, t.p, a, :], cb_y1[:, t.p, a, :], ACT.Copy,
                                          scale=w1[:, bass.ds(2 * t.n + a, 1), :].rearrange("p a b -> p (a b)"))
                last.then_inc(cb_act.sem, 1)

            sweep(act, NT // 2, *in_turn((first_product, 0)))

        @block.vector
        def _(dve):
            def split_lo(i):
                w = ORDER[i]
                dve.wait_ge(wsplit_hi, i + 1)
                dve.tensor_tensor(flat(lo[w][:]), staged[i], flat(hi[w][:]).bitcast(F32),
                                  ALU.subtract).then_inc(wsplit_lo, 1)

            def mod_row(m):
                dve.wait_ge(mod_mm, m + 1)
                step = MOD_AT[m - 1] if m else 0
                if m in (GA, GB):
                    dve.wait_ge(mod_vec, step)
                    dve.tensor_scalar(gate_sign, psum[m][0:B, :], 0.0, 2.0, ALU.is_ge, ALU.mult).then_inc(mod_vec, 1)
                    dve.tensor_scalar(gate_neg, psum[m][0:B, :], -1.0, 0.25, ALU.mult, ALU.max).then_inc(mod_vec, 1)
                    dve.wait_ge(mod_vec, step + 2)
                    dve.tensor_scalar(gate_sign, gate_sign, -1.0, None, ALU.add).then_inc(mod_vec, 1)
                    dve.tensor_tensor(gate_neg, psum[m][0:B, :], gate_neg, ALU.max).then_inc(mod_vec, 1)
                    dve.wait_ge(mod_vec, step + 4)
                    dve.tensor_tensor(mod_rows[m], gate_sign, gate_neg, ALU.mult).then_inc(mod_vec, 1)
                else:
                    dve.tensor_scalar(mod_rows[m], psum[m][0:B, :], 1.0 if m in (CA, CB) else 0.0, None,
                                      ALU.add).then_inc(mod_vec, 1)

            SA, CA, GA, SB, CB, GB = range(6)
            split_lo(0)
            split_lo(1)
            mod_row(SA)
            mod_row(CA)
            mod_row(GA)
            split_lo(2)
            mod_row(SB)
            mod_row(CB)
            mod_row(GB)
            split_lo(3)
            dve.wait_ge(const_ready, CONSTS)
            dve.wait_ge(mod_vec, MOD_DONE)
            dve.wait_ge(mod1_in, 16 * B)

            def split_staged(t):
                if t.pair is None and t.n == 0:
                    for i in range(len(W1), NW - 1):
                        split_lo(i)
                    dve.wait_ge(wsplit_lo, NW - 1)

            def split_last(t):
                if t.pair is None and t.n == 0:
                    split_lo(NW - 1)
                    dve.wait_ge(wsplit_hi, NW + 1)
                    dve.tensor_tensor(wrt_lo, wrt[:], wrt_hi.bitcast(F32), ALU.subtract).then_inc(wsplit_lo, 1)
                    dve.wait_ge(u_in, 16)
                    dve.wait_ge(wsplit_lo, NW + 1)
                    dve.tensor_scalar(u_bc[:], u_bc[:], LN_1E8, None, ALU.add).then_inc(u_ready, 1)
                    dve.wait_ge(u_ready, 1)

            def x_stats(t):
                dve.wait_ge(x_in[t.p], 16 * t.half + 16)
                dve.bn_stats(st1[:, t.p, :], x_t[:, t.p, :]).then_inc(lnx_vec.sem, 1)

            def x_moments(t):
                bridge(dve, 0, lnx_vec.done(t.n, "stats"))
                dve.bn_aggr(mv1[:, t.p, :], st1[:, t.p, :]).then_inc(lnx_vec.sem, 1)

            def scaled(t):
                batch = t.n // TPB
                dve.wait_ge(*lnx_vec.done(t.n, "moments"))
                dve.scalar_tensor_tensor(xh[:], x_t[:, t.p, :], mv1[:, t.p, 0:1],
                                         mod1[:, bass.ds(batch, 1), 1, :].rearrange("p a d -> p (a d)"), ALU.subtract,
                                         ALU.mult).then_inc(lnh_vec.sem, 1)

            def h_of(t):
                batch = t.n // TPB
                if t.back(2).real():
                    dve.wait_ge(h_out[t.p], 16 * t.half)
                elif t.n == 0:
                    dve.wait_ge(mod_out, 96)
                dve.wait_ge(*lnx_pool.done(t.n, "rstd"))
                dve.wait_ge(*lnh_vec.done(t.n, "scaled"))
                dve.scalar_tensor_tensor(h_t[:, t.p, :], xh[:], rstd1[:, t.p, :],
                                         mod1[:, bass.ds(batch, 1), 0, :].rearrange("p a d -> p (a d)"), ALU.mult,
                                         ALU.add).then_inc(lnh_vec.sem, 1)

            def h_stats(t):
                dve.wait_ge(*lnh_vec.done(t.n, "h"))
                dve.bn_stats(st1h[:, t.p, :], h_t[:, t.p, :]).then_inc(lnh_vec.sem, 1)

            def h_moments(t):
                bridge(dve, 1, lnh_vec.done(t.n, "stats"))
                dve.bn_aggr(mv1h[:, t.p, :], st1h[:, t.p, :]).then_inc(lnh_vec.sem, 1)

            def hhat(t):
                if t.back(2).real():
                    dve.wait_ge(*t1_pe.done(t.back(2).n, "turned"))
                dve.wait_ge(*lnh_pool.done(t.n, "rstd"))
                dve.tensor_scalar(hh[:, t.p, :], h_t[:, t.p, :], mv1h[:, t.p, 0:1], rstd1h[:, t.p, :], ALU.subtract,
                                  ALU.mult).then_inc(hh_vec.sem, 1)

            def first_col(t):
                if t.back(1).real():
                    dve.wait_ge(*h1T_act.done(t.back(1).n, "h1T"))
                dve.tensor_tensor(h1T[:, t.p, :, 0:1], h1T[:, 1 - t.p, :, P:P + 1],
                                  keep[:, bass.ds(t.n * C, C)].unsqueeze(2), ALU.mult).then_inc(mix_vec.sem, 1)

            def mixes(t):
                if t.back(1).real():
                    dve.wait_ge(*mix_act.done(t.back(1).n, "mix_hi"))
                dve.wait_ge(*mix_pool.done(t.n, "diff"))
                for m, mu in enumerate((MUR, MUK, MUV)):
                    for c in range(C):
                        last = dve.scalar_tensor_tensor(mix1[:, m, c, :], diff1[:, c, :], vecs[:, mu, c:c + 1],
                                                        h1T[:, t.p, c, 0:P], ALU.mult, ALU.add)
                last.then_inc(mix_vec.sem, 1)

            def mix_lo(t):
                dve.wait_ge(*mix_act.done(t.n, "mix_hi"))
                dve.tensor_tensor(xm_lo[:, t.p].rearrange("p m c t -> p (m c t)"), stage[0][:, 0:3 * D],
                                  xm_hi[:, t.p].rearrange("p m c t -> p (m c t)").bitcast(F32),
                                  ALU.subtract).then_inc(mix_vec.sem, 1)

            def z_of(t):
                if t.back(1).real():
                    dve.wait_ge(*sk_act.done(t.back(1).n, "sk"))
                dve.wait_ge(*rkv_pe.done(t.n, "k"))
                dve.tensor_tensor(z_t, PS_K[:], u_bc[:], ALU.add).then_inc(post_vec.sem, 1)

            def vk_of(t):
                dve.wait_ge(*rkv_pe.done(t.n, "v"))
                if t.back(1).real():
                    dve.wait_ge(*rw_pool.done(t.back(1).n, "rw"))
                dve.wait_ge(*sk_act.done(t.n, "sk"))
                dve.tensor_tensor(vk_t, PS_V[t.p][:], sk_t, ALU.mult).then_inc(post_vec.sem, 1)

            def rwlo(t):
                dve.wait_ge(*rw_act.done(t.n, "rw_hi"))
                dve.tensor_tensor(flat(rw_lo[:]), PS_TR[:], flat(rw_hi[:]).bitcast(F32),
                                  ALU.subtract).then_inc(rw_vec.sem, 1)

            sweep(dve, NT, *in_turn((first_col, -1), (z_of, 1), (x_stats, -4), (scaled, -3), (hhat, -2), (h_of, -3),
                                    (x_moments, -4), (split_last, -1), (mixes, -1), (h_stats, -3), (vk_of, 1), (rwlo, 2),
                                    (h_moments, -3), (split_staged, -3),
                                    (mix_lo, -1)))

            wait_h_rows(dve)
            dve.wait_ge(const_ready, CONSTS + 1)

            def stats_2(t):
                dve.wait_ge(*x2_pool.done(t.n, "x2"))
                dve.bn_stats(st2[:, t.p, :], x2_t[:, t.p, :]).then_inc(ln2_vec.sem, 1)

            def moments_2(t):
                bridge(dve, 2, ln2_vec.done(t.n, "stats"))
                dve.bn_aggr(mv2[:, t.p, :], st2[:, t.p, :]).then_inc(ln2_vec.sem, 1)

            def xhat_2(t):
                if t.back(2).real():
                    dve.wait_ge(*t2_pe.done(t.back(2).n, "turned"))
                dve.wait_ge(*ln2_pool.done(t.n, "rstd"))
                dve.tensor_scalar(xh2[:, t.p, :], x2_t[:, t.p, :], mv2[:, t.p, 0:1], rstd2[:, t.p, :], ALU.subtract,
                                  ALU.mult).then_inc(xh2_vec.sem, 1)

            def first_col_2(t):
                if t.back(1).real():
                    dve.wait_ge(*h2T_act.done(t.back(1).n, "h2T"))
                dve.tensor_tensor(h2T[:, t.p, :, 0:1], h2T[:, 1 - t.p, :, P:P + 1],
                                  keep[:, bass.ds(t.n * C, C)].unsqueeze(2), ALU.mult).then_inc(mix2_vec.sem, 1)

            def mixes_2(t):
                if t.back(1).real():
                    dve.wait_ge(*mix2_act.done(t.back(1).n, "mix_hi"))
                dve.wait_ge(*mix2_pool.done(t.n, "diff"))
                for m, mu in enumerate((MUR2, MUK2)):
                    for c in range(C):
                        last = dve.scalar_tensor_tensor(mix2[:, m, c, :], diff2[:, c, :], vecs[:, mu, c:c + 1],
                                                        h2T[:, t.p, c, 0:P], ALU.mult, ALU.add)
                last.then_inc(mix2_vec.sem, 1)

            def mix_lo_2(t):
                dve.wait_ge(*mix2_act.done(t.n, "mix_hi"))
                dve.tensor_tensor(xm2_lo[:, t.p].rearrange("p m c t -> p (m c t)"),
                                  mix2[:].rearrange("p m c t -> p (m c t)"),
                                  xm2_hi[:, t.p].rearrange("p m c t -> p (m c t)").bitcast(F32),
                                  ALU.subtract).then_inc(mix2_vec.sem, 1)

            def k2lo(t):
                dve.wait_ge(*tk_act.done(t.n, "k2_hi"))
                dve.tensor_tensor(flat(k2_lo[:]), PS_TK[:], flat(k2_hi[:]).bitcast(F32),
                                  ALU.subtract).then_inc(tk_vec.sem, 1)

            def y_of(t):
                if t.back(1).real():
                    dve.wait_ge(*res_pool.done(t.back(1).n, "xres"))
                dve.wait_ge(*tk_pe.done(t.n, "cv"))
                dve.wait_ge(*post2_act.done(t.n, "sr2"))
                dve.tensor_tensor(y_t[:], PS_CV[:], sr2[:, t.p, :], ALU.mult).then_inc(y_vec.sem, 1)

            def stats_3(t):
                dve.wait_ge(*res_pool.done(t.n, "xres"))
                dve.bn_stats(st3[:, t.p, :], xr_t[:, t.p, :]).then_inc(ln3_vec.sem, 1)

            def moments_3(t):
                bridge(dve, 3, ln3_vec.done(t.n, "stats"))
                dve.bn_aggr(mv3[:, t.p, :], st3[:, t.p, :]).then_inc(ln3_vec.sem, 1)

            def scaled_3(t):
                batch = t.n // TPB
                if t.back(2).real():
                    dve.wait_ge(h3_out[t.p], 16 * t.half)
                    dve.wait_ge(*t3_pe.done(t.back(2).n, "turned"))
                if t.pair is None and t.n == 0:
                    dve.wait_ge(mod2_in, 16 * B)
                dve.wait_ge(*ln3_vec.done(t.n, "moments"))
                dve.scalar_tensor_tensor(h3_t[:, t.p, :], xr_t[:, t.p, :], mv3[:, t.p, 0:1],
                                         mod2[:, bass.ds(batch, 1), 2, :].rearrange("p a d -> p (a d)"), ALU.subtract,
                                         ALU.mult).then_inc(ln3_vec.sem, 1)

            def h3_of(t):
                batch = t.n // TPB
                dve.wait_ge(*ln3_pool.done(t.n, "rstd"))
                dve.wait_ge(*ln3_vec.done(t.n, "scaled"))
                dve.scalar_tensor_tensor(h3_t[:, t.p, :], h3_t[:, t.p, :], rstd3[:, t.p, :],
                                         mod2[:, bass.ds(batch, 1), 1, :].rearrange("p a d -> p (a d)"), ALU.mult,
                                         ALU.add).then_inc(ln3_vec.sem, 1)

            def h3lo(t):
                dve.wait_ge(*t3_act.done(t.n, "h3_hi"))
                dve.tensor_tensor(flat(h3_lo[:]), PS_T3[:], flat(h3_hi[:]).bitcast(F32),
                                  ALU.subtract).then_inc(t3_vec.sem, 1)

            def logits_out(t):
                dve.wait_ge(*t3_pe.done(t.n, "logits"))
                dve.tensor_scalar(lg_part[:, t.p, :], PS_LG[:, 0:8], 1.0, None, ALU.mult).then_inc(lg_vec.sem, 1)
                dve.wait_ge(*lg_vec.done(t.n, "part"))
                dve.tensor_tensor(logits[:, bass.ds(t.n, 1), :].rearrange("p a e -> p (a e)"), lg_part[:, t.p, :],
                                  PS_LG[:, 8:16], ALU.add).then_inc(lg_vec.sem, 1)

            def pads(t):
                if t.pair is None and t.n == 0:
                    wait_a1(dve)
                    for i in range(2):
                        dve.memset(raw[i][F % P:P, RAW - D:RAW], 0.0).then_inc(pad_ready, 1)
                    dve.memset(hid[:, :, F:FK * P], 0.0).then_inc(pad_ready, 1)

            def x_lo(slot, number, act_steps, vec_steps):
                dve.wait_ge(*act_steps.done(number, "hi"))
                dve.tensor_tensor(flat(ex_x_lo[:, slot]), PS_X[:], flat(ex_x_hi[:, slot]).bitcast(F32),
                                  ALU.subtract).then_inc(vec_steps.sem, 1)

            def split_gu(i):
                dve.wait_ge(sh_split_hi, i + 1)
                dve.tensor_tensor(flat(gu_lo[i][:]), raw[i][:, 0:C * GU], flat(gu_hi[i][:]).bitcast(F32),
                                  ALU.subtract).then_inc(sh_split_lo, 1)

            def split_dn(i):
                dve.wait_ge(sh_split_hi, i + 3)
                dve.tensor_tensor(flat(dn_lo[i][:]), raw[i][:, C * GU:RAW], flat(dn_hi[i][:]).bitcast(F32),
                                  ALU.subtract).then_inc(sh_split_lo, 1)

            def first_shared(t):
                if t.pair is None and t.n == NT - 1:
                    x_lo(0, 0, shx_act, shx_vec)
                    dve.wait_ge(*rk2_pe.done(t.n, "k2"))
                    split_gu(0)

            sweep(dve, NT, *in_turn((pads, 1), (y_of, 2), (logits_out, 5), (first_col_2, -1), (stats_3, 3), (stats_2, -3), (moments_3, 3), (xhat_2, -2),
                                    (moments_2, -3), (mixes_2, -1), (h3lo, 4), (k2lo, 1), (mix_lo_2, -1), (scaled_3, 3),
                                    (h3_of, 3), (first_shared, 4)))

            wait_a2(dve)
            taken = [0]

            def link(instruction):
                taken[0] += 1
                instruction.then_inc(route_vec, 1)
                dve.wait_ge(route_vec, taken[0])

            def over_e(ap):
                return ap.to_broadcast([P, NT, E])

            def logits_less_max():
                link(dve.tensor_reduce(row["mx"][:, :, 0], logits[:], AX.X, ALU.max))
                link(dve.tensor_tensor(route["ex"][:], logits[:], over_e(row["mx"][:]), ALU.subtract))

            def best(w, hot):
                link(dve.tensor_reduce(w[:, :, 0], route["sc"][:], AX.X, ALU.max))
                link(dve.tensor_tensor(route["tmp"][:], route["sc"][:], over_e(w[:]), ALU.is_equal))
                link(dve.tensor_tensor(route["tmp"][:], route["tmp"][:], iota_e[:], ALU.mult))
                link(dve.tensor_reduce(row["pick"][:, :, 0], route["tmp"][:], AX.X, ALU.min))
                link(dve.tensor_tensor(route[hot][:], iota_e[:], over_e(row["pick"][:]), ALU.is_equal))

            def softmax_and_first():
                dve.wait_ge(route_exp, 1)
                link(dve.tensor_reduce(row["sum"][:, :, 0], route["ex"][:], AX.X, ALU.add))
                link(dve.reciprocal(row["rec"][:], row["sum"][:]))
                link(dve.tensor_tensor(route["sc"][:], route["ex"][:], over_e(row["rec"][:]), ALU.mult))
                dve.wait_ge(ex_const, 3)
                best(w1, "oh1")

            def second():
                link(dve.scalar_tensor_tensor(flat(route["sc"][:]), flat(route["oh1"][:]), -2.0, flat(route["sc"][:]),
                                              ALU.mult, ALU.add))
                best(w2, "oh2")
                link(dve.tensor_tensor(route["both"][:], route["oh1"][:], route["oh2"][:], ALU.add))
                assert taken[0] == ROUTE_BOTH

            def running_sum(where, names, parts, piece):
                cur, nxt = names
                reach = 1
                while reach < parts:
                    link(dve.tensor_copy(piece(where[nxt], 0, reach), piece(where[cur], 0, reach)))
                    link(dve.tensor_tensor(piece(where[nxt], reach, parts), piece(where[cur], reach, parts),
                                           piece(where[cur], 0, parts - reach), ALU.add))
                    cur, nxt = nxt, cur
                    reach *= 2
                return cur

            def earlier_tiles():
                dve.wait_ge(route_pe, 1)
                link(dve.tensor_copy(route["cur"][:], PS_TOT))
                cur = running_sum(route, ("cur", "nxt"), NT, lambda ap, a, b: ap[:, a:b, :])
                link(dve.tensor_copy(count["total"][:], route[cur][:, NT - 1:NT, :]))
                link(dve.tensor_tensor(route["pos"][:], route[cur][:], PS_TOT, ALU.subtract))

            def padded_counts():
                link(dve.tensor_tensor(route["pos"][:], route["pos"][:], PS_PRE, ALU.add))
                link(dve.tensor_scalar(count_i[:], flat(count["total"][:]), float(R - 1), None, ALU.add))
                link(dve.tensor_scalar(count_i[:], count_i[:], -R, None, ALU.bitwise_and))
                link(dve.tensor_copy(flat(count["padded"][:]), count_i[:]))
                link(dve.tensor_copy(count["end"][:], count["padded"][:]))
                cur = running_sum(count, ("end", "end2"), E, lambda ap, a, b: ap[:, :, a:b])
                assert cur == "end2"

            def row_slots():
                link(dve.tensor_tensor(count["start"][:], count["end2"][:], count["padded"][:], ALU.subtract))
                link(dve.tensor_tensor(route["pos"][:], route["pos"][:], count["start"][:].to_broadcast([P, NT, E]), ALU.add))
                for k, hot in enumerate(("oh1", "oh2")):
                    link(dve.tensor_tensor(route["tmp"][:], route[hot][:], route["pos"][:], ALU.mult))
                    link(dve.tensor_reduce(row["s1"][:, :, 0], route["tmp"][:], AX.X, ALU.add))
                    link(dve.tensor_copy(slots[:, k, :], row["s1"][:, :, 0]))

            def tile_experts():
                link(dve.tensor_tensor(below[:], count["end2"][:].to_broadcast([P, NJ, E]), first_row[:], ALU.is_le))
                link(dve.tensor_reduce(eid_f[:, :, 0], below[:], AX.X, ALU.add))
                link(dve.tensor_scalar(eid_f[:], eid_f[:], float(E - 1), None, ALU.min))
                dve.tensor_copy(eid[:], eid_f[:, :, 0]).then_inc(route_done, 1)

            ROUTING = {0: softmax_and_first, 1: second, 3: earlier_tiles, 4: padded_counts, 5: row_slots, 6: tile_experts}

            dve.wait_ge(mod3_in, 16 * B)
            dve.wait_ge(pad_ready, 3)

            def hid_of(u, pe_steps, act_steps, vec_steps, first):
                if not first:
                    dve.wait_ge(*pe_steps.done(u.back(2).n, "turned"))
                elif pe_steps is ru_pe:
                    dve.wait_ge(*shu_pe.done(LAST.unit(u.half).n, "turned"))
                dve.wait_ge(*act_steps.done(u.n, "silu"))
                dve.tensor_tensor(hid[:, u.half, 0:F], PS_U[u.half][:, 0:F], sg_t[:], ALU.mult).then_inc(vec_steps.sem_of["hid"], 1)

            def hidlo(u, act_steps, vec_steps):
                dve.wait_ge(*act_steps.done(u.n, "hid_hi"))
                dve.tensor_tensor(flat(hid_lo[:]), PS_H[:, 0:FK * P], flat(hid_hi[:]).bitcast(F32),
                                  ALU.subtract).then_inc(vec_steps.sem_of["hid_lo"], 1)

            def base_of(t):
                batch = t.n // TPB
                dve.wait_ge(*shu_pe.done(t.unit(1).n, "down"))
                if t.back(1).real():
                    dve.wait_ge(*base_vec.done(t.back(1).n, "base"))
                dve.tensor_tensor(gated_t[:], PS_Y[:], mod3[:, bass.ds(batch, 1), :].rearrange("p a d -> p (a d)"),
                                  ALU.mult).then_inc(base_vec.sem, 1)
                rows = base[:, bass.ds(t.n, 1), :].rearrange("p a d -> p (a d)")
                dve.wait_ge(sr_in[t.p], 16 * t.half + 16)
                dve.wait_ge(*base_vec.done(t.n, "gated"))
                dve.tensor_tensor(rows, rows, gated_t[:], ALU.add).then_inc(base_vec.sem, 1)

            def expert_lo(t, part):
                w_hi, w_lo = (gu_hi, gu_lo) if part == 0 else (dn_hi, dn_lo)
                cols = slice(0, C * GU) if part == 0 else slice(C * GU, RAW)
                dve.wait_ge(*rw_hi_act.done(t.n, "gu_hi" if part == 0 else "dn_hi"))
                dve.tensor_tensor(flat_of(w_lo, t), raw[t.p][:, cols], flat_of(w_hi, t).bitcast(F32),
                                  ALU.subtract).then_inc(rw_lo_vec.sem, 1)

            def shared_step(t):
                if t.real() and t.back(-1).real():
                    x_lo(t.back(-1).p, t.back(-1).n, shx_act, shx_vec)
                if t.pair is None and t.n == -1:
                    logits_less_max()
                    split_gu(1)
                    split_dn(0)
                    split_dn(1)
                for half in range(2):
                    before = t if half else t.back(1)
                    if before.real():
                        hidlo(before.unit(1 - half), shu_act, shu_vec)
                    if t.pair is None and t.n == NT - 1 and half:
                        expert_lo(FIRST, 0)
                    if t.real():
                        hid_of(t.unit(half), shu_pe, shu_act, shu_vec, not t.back(1).real())
                    if half == 0 and before.real():
                        base_of(before)
                    if t.pair is None and t.real() and t.unit(half).n in ROUTING:
                        ROUTING[t.unit(half).n]()
                if t.pair is None and t.n == NT - 1:
                    for p in range(2):
                        dve.wait_ge(sc_out[p], 32 * (NT // 2))
                    x_lo(0, 0, rx_act, rx_vec)

            sweep(dve, NT, 1, 1, shared_step)

            def y_of_unit(u, t):
                if t.back(1).real():
                    dve.wait_ge(ys_out[u.half], 16 * t.n)
                dve.wait_ge(*ru_pe.done(u.n, "down"))
                dve.tensor_copy(y_rows[:, u.half, :], PS_Y[:]).then_inc(ru_vec.sem_of["y"], 1)

            def routed_step(t):
                for half in range(2):
                    before = t if half else t.back(1)
                    if half and t.back(-1).real() and t.real():
                        x_lo(0, t.back(-1).unit(0).n, rx_act, rx_vec)
                    if not half and t.real():
                        x_lo(1, t.unit(1).n, rx_act, rx_vec)
                    if before.real():
                        hidlo(before.unit(1 - half), ru_act, ru_vec)
                    if t.real():
                        hid_of(t.unit(half), ru_pe, ru_act, ru_vec, not t.back(1).real())
                    if t.back(-1).real() and not (t.pair is None and t.n == -1 and half == 0):
                        expert_lo(t.back(-1), half)
                    if before.real():
                        y_of_unit(before.unit(1 - half), before)

            sweep(dve, NJ, 1, 1, routed_step)

            wait_routed(dve)

            def combine(t):
                batch = t.n // (TPB // 2)
                dve.wait_ge(y2_in[t.p], 32 * t.half + 32)
                dve.wait_ge(*cb_act.done(t.n, "first"))
                for a in range(2):
                    last = dve.scalar_tensor_tensor(cb_out[:, t.p, a, :], cb_y2[:, t.p, a, :],
                                                    w2[:, bass.ds(2 * t.n + a, 1), :].rearrange("p a b -> p (a b)"),
                                                    cb_out[:, t.p, a, :], ALU.mult, ALU.add)
                last.then_inc(cb_vec.sem, 1)
                dve.wait_ge(*cb_vec.done(t.n, "both"))
                dve.tensor_tensor(cb_out[:, t.p], cb_out[:, t.p], mod3[:, bass.ds(batch, 1), :].to_broadcast([P, 2, D]),
                                  ALU.mult).then_inc(cb_vec.sem, 1)
                dve.wait_ge(*cb_vec.done(t.n, "gated"))
                dve.tensor_tensor(cb_out[:, t.p], cb_out[:, t.p], base[:, bass.ds(2 * t.n, 2), :],
                                  ALU.add).then_inc(cb_vec.sem, 1)

            sweep(dve, NT // 2, *in_turn((combine, 0)))

        @block.tensor
        def _(pe):
            pe.wait_ge(silu_c, 1)
            for m in range(6):
                if m % 2 == 0:
                    pe.wait_ge(wmod_in[m // 2], 16 * C)
                for c in range(C):
                    last = pe.matmul(psum[m][0:B, :], cT[:, c, :], wmod[:, c, m * D:(m + 1) * D], start=(c == 0),
                                     stop=(c == C - 1))
                last.then_inc(mod_mm, 1)
            pe.wait_ge(const_ready, CONSTS)
            pe.wait_ge(mod_vec, MOD_DONE)

            def t1(t):
                if t.back(1).real():
                    pe.wait_ge(*h1T_act.done(t.back(1).n, "h1T"))
                pe.wait_ge(*hh_vec.done(t.n, "hhat"))
                turn(pe, PS_T1, hh[:, t.p, :]).then_inc(t1_pe.sem, 1)

            def mixed_product(t, m, w, bank):
                return product(pe, bank[:], chunks_of(xm_hi[:, t.p, m]), chunks_of(xm_lo[:, t.p, m]),
                               chunks_of(hi[w]), chunks_of(lo[w]))

            def r(t):
                if t.back(1).real():
                    pe.wait_ge(*sr_act.done(t.back(1).n, "sr"))
                if t.pair is None and t.n == 0:
                    pe.wait_ge(wsplit_lo, NW + 1)
                pe.wait_ge(*mix_vec.done(t.n, "mix_lo"))
                mixed_product(t, 0, "r", PS_R).then_inc(rkv_pe.sem, 1)

            def k(t):
                if t.back(1).real():
                    pe.wait_ge(*post_vec.done(t.back(1).n, "z"))
                mixed_product(t, 1, "k", PS_K).then_inc(rkv_pe.sem, 1)

            def v(t):
                if t.back(2).real():
                    pe.wait_ge(*post_vec.done(t.back(2).n, "vk"))
                mixed_product(t, 2, "v", PS_V[t.p]).then_inc(rkv_pe.sem, 1)

            def trw(t):
                if t.back(1).real():
                    pe.wait_ge(*rw_vec.done(t.back(1).n, "rw_lo"))
                pe.wait_ge(*rw_pool.done(t.n, "rw"))
                turn(pe, PS_TR, rw_t).then_inc(rw_pe.sem, 1)

            def o(t):
                if t.back(1).real():
                    pe.wait_ge(*o_act.done(t.back(1).n, "o"))
                pe.wait_ge(*rw_vec.done(t.n, "rw_lo"))
                product(pe, PS_O[:], chunks_of(rw_hi), chunks_of(rw_lo), chunks_of(hi["o"]),
                        chunks_of(lo["o"])).then_inc(rw_pe.sem, 1)

            sweep(pe, NT, *in_turn((r, 0), (trw, 2), (k, 0), (t1, -2), (v, 0), (o, 2)))

            def t2(t):
                if t.back(1).real():
                    pe.wait_ge(*h2T_act.done(t.back(1).n, "h2T"))
                pe.wait_ge(*xh2_vec.done(t.n, "xhat"))
                turn(pe, PS_T2, xh2[:, t.p, :]).then_inc(t2_pe.sem, 1)

            def r2(t):
                if t.back(1).real():
                    pe.wait_ge(*post2_act.done(t.back(1).n, "sr2"))
                pe.wait_ge(*mix2_vec.done(t.n, "mix_lo"))
                product(pe, PS_R2[:], chunks_of(xm2_hi[:, t.p, 0]), chunks_of(xm2_lo[:, t.p, 0]), chunks_of(hi["r2"]),
                        chunks_of(lo["r2"])).then_inc(rk2_pe.sem, 1)

            def k2(t):
                if t.back(1).real():
                    pe.wait_ge(*post2_act.done(t.back(1).n, "relu"))
                product(pe, PS_K2[:], chunks_of(xm2_hi[:, t.p, 1]), chunks_of(xm2_lo[:, t.p, 1]), chunks_of(hi["k2"]),
                        chunks_of(lo["k2"])).then_inc(rk2_pe.sem, 1)

            def tk(t):
                if t.back(1).real():
                    pe.wait_ge(*tk_vec.done(t.back(1).n, "k2_lo"))
                pe.wait_ge(*post2_act.done(t.n, "k2"))
                turn(pe, PS_TK, k2_t).then_inc(tk_pe.sem, 1)

            def cv(t):
                if t.back(1).real():
                    pe.wait_ge(*y_vec.done(t.back(1).n, "y"))
                pe.wait_ge(*tk_vec.done(t.n, "k2_lo"))
                product(pe, PS_CV[:], chunks_of(k2_hi), chunks_of(k2_lo), chunks_of(hi["v2"]),
                        chunks_of(lo["v2"])).then_inc(tk_pe.sem, 1)

            def t3(t):
                if t.back(1).real():
                    pe.wait_ge(*t3_vec.done(t.back(1).n, "h3_lo"))
                pe.wait_ge(*ln3_vec.done(t.n, "h3"))
                turn(pe, PS_T3, h3_t[:, t.p, :]).then_inc(t3_pe.sem, 1)

            def router(t):
                if t.back(1).real():
                    pe.wait_ge(*lg_vec.done(t.back(1).n, "copied"))
                pe.wait_ge(*t3_vec.done(t.n, "h3_lo"))
                for c in range(C):
                    pe.matmul(PS_LG[:, 0:16], h3_hi[:, c, :], wrt_hl[:, c, :], start=c == 0, stop=False)
                    last = pe.matmul(PS_LG[:, 0:16], h3_lo[:, c, :], wrt_hl[:, c, :], start=False, stop=c == C - 1)
                last.then_inc(t3_pe.sem, 1)

            def turn_shared(t):
                if t.back(1).real():
                    pe.wait_ge(*shx_vec.done(t.back(1).n, "lo"))
                pe.wait_ge(sx_in[t.p], 16 * t.half + 16)
                turn(pe, PS_X, ex_x[:, t.p, :]).then_inc(shx_pe.sem, 1)

            def first_shared(t):
                if t.pair is None and t.n == NT - 1:
                    pe.wait_ge(*post2_act.done(t.n, "sr2"))
                    turn_shared(Tile(None, 0, NT))

            sweep(pe, NT, *in_turn((r2, 0), (tk, 1), (t3, 4), (k2, 0), (t2, -2), (router, 4), (cv, 1), (first_shared, 3)))


            def route_counts():
                pe.wait_ge(route_vec, ROUTE_BOTH)
                hot = flat(route["both"][:])
                pe.matmul(PS_RT[:, 0:NT * E], earlier[:], hot, start=True, stop=True)
                pe.matmul(PS_RT[:, NT * E:2 * NT * E], ones[:], hot, start=True, stop=True).then_inc(route_pe, 1)

            def up(u, x_slot, w, first, pe_steps, vec_steps):
                if not first:
                    pe.wait_ge(*vec_steps.done(u.back(2).n, "hid"))
                elif pe_steps is ru_pe:
                    pe.wait_ge(*shu_vec.done(LAST.unit(u.half).n, "hid"))
                for bank, col in ((PS_G[u.half], 0), (PS_U[u.half], F)):
                    last = product(pe, bank[:, 0:F], chunks_of(ex_x_hi[:, x_slot]), chunks_of(ex_x_lo[:, x_slot]),
                                   [gu_hi[w][:, c, col:col + F] for c in range(C)],
                                   [gu_lo[w][:, c, col:col + F] for c in range(C)])
                last.then_inc(pe_steps.sem_of["up"], 1)

            def turn_hid(u, first, pe_steps, vec_steps):
                if not first:
                    pe.wait_ge(*vec_steps.done(u.back(1).n, "hid_lo"))
                elif pe_steps is ru_pe:
                    pe.wait_ge(*shu_vec.done(LAST_UNIT.n, "hid_lo"))
                pe.wait_ge(*vec_steps.done(u.n, "hid"))
                for c in range(FK):
                    last = pe.transpose(PS_H[:, c * P:(c + 1) * P], hid[:, u.half, c * P:(c + 1) * P], ident[:])
                last.then_inc(pe_steps.sem_of["turned"], 1)

            def down(u, w, start, stop, pe_steps, vec_steps):
                pe.wait_ge(*vec_steps.done(u.n, "hid_lo"))
                for c in range(FK):
                    pe.matmul(PS_Y[:], hid_hi[:, c, :], dn_hi[w][:, c, :], start=start and c == 0, stop=False)
                    pe.matmul(PS_Y[:], hid_hi[:, c, :], dn_lo[w][:, c, :], start=False, stop=False)
                    last = pe.matmul(PS_Y[:], hid_lo[:, c, :], dn_hi[w][:, c, :], start=False, stop=stop and c == FK - 1)
                last.then_inc(pe_steps.sem_of["down"], 1)

            def turn_rows(t, half, first):
                u = t.unit(half)
                if not first:
                    pe.wait_ge(*rx_vec.done(u.back(1).n, "lo"))
                else:
                    pe.wait_ge(*shx_vec.done(NT - 1, "lo"))
                pe.wait_ge(ex_in[half], 16 * t.n + 16)
                turn(pe, PS_X, ex_x[:, half, :]).then_inc(rx_pe.sem, 1)

            def shared_step(t):
                if t.real() and t.back(-1).real():
                    turn_shared(t.back(-1))
                for half in range(2):
                    before = t if half else t.back(1)
                    u = before.unit(1 - half)
                    if before.real():
                        turn_hid(u, not before.back(1).real() and half, shu_pe, shu_vec)
                    if t.real():
                        if half == 0:
                            pe.wait_ge(*shx_vec.done(t.n, "lo"))
                        if t.pair is None and t.n == 0:
                            pe.wait_ge(sh_split_lo, half + 1)
                        up(t.unit(half), t.p, half, not t.back(1).real(), shu_pe, shu_vec)
                    if t.pair is None and t.n == 1 and half == 1:
                        route_counts()
                    if before.real():
                        if half and before.back(1).real():
                            pe.wait_ge(*base_vec.done(before.back(1).n, "gated"))
                        if t.pair is None and before.n == 0:
                            pe.wait_ge(sh_split_lo, 1 - half + 3)
                        down(u, 1 - half, half == 1, half == 0, shu_pe, shu_vec)
                if t.pair is None and t.n == NT - 1:
                    turn_rows(FIRST, 0, True)

            sweep(pe, NT, 1, 1, shared_step)

            def routed_step(t):
                for half in range(2):
                    before = t if half else t.back(1)
                    if half and t.back(-1).real() and t.real():
                        turn_rows(t.back(-1), 0, False)
                    if not half and t.real():
                        turn_rows(t, 1, False)
                    u = before.unit(1 - half)
                    if before.real():
                        turn_hid(u, not before.back(1).real() and half, ru_pe, ru_vec)
                    if t.real():
                        pe.wait_ge(*rx_vec.done(t.unit(half).n, "lo"))
                        if half == 0:
                            pe.wait_ge(*rw_lo_vec.done(t.n, "gu_lo"))
                        up(t.unit(half), half, t.p, not t.back(1).real(), ru_pe, ru_vec)
                    if before.real():
                        if half == 0 or before.back(1).real():
                            pe.wait_ge(*ru_vec.done(u.back(1).n, "y"))
                        else:
                            pe.wait_ge(*base_vec.done(NT - 1, "gated"))
                        if half:
                            pe.wait_ge(*rw_lo_vec.done(before.n, "dn_lo"))
                        down(u, before.p, True, True, ru_pe, ru_vec)

            sweep(pe, NJ, 1, 1, routed_step)



def kernel(**inputs):
    import numpy as np
    import concourse.bacc as bacc
    from concourse.bass_utils import run_bass_kernel_spmd as run

    def a(name):
        return np.asarray(inputs["L0_" + name])

    arrays = {"x": a("attn_x"), "cT": a("c").T, "wmod": a("wmod"), "u": a("attn_tm_u"), "wrT": a("ffn_Wr").T}
    for mine, name in (("ln1_g", "ln1_g"), ("ln1_b", "ln1_b"), ("ln2_g", "ln2_g"), ("ln2_b", "ln2_b"),
                       ("mu_r", "tm_mu_r"), ("mu_k", "tm_mu_k"), ("mu_v", "tm_mu_v"), ("mu_r2", "cm_mu_r"),
                       ("mu_k2", "cm_mu_k")):
        arrays[mine] = a("attn_" + name)
    for mine, name in (("w_r", "tm_Wr"), ("w_k", "tm_Wk"), ("w_v", "tm_Wv"), ("w_o", "tm_Wout"), ("w_r2", "cm_Wr"),
                       ("w_k2", "cm_Wk"), ("w_v2", "cm_Wv")):
        arrays[mine] = a("attn_" + name).T

    def gate_up(gate, up):
        both = np.concatenate([gate.transpose(0, 2, 1), up.transpose(0, 2, 1)], axis=2)
        return both.reshape(-1, C, P, GU).transpose(0, 2, 1, 3).reshape(-1, P, C * GU)

    arrays["sh_gu"] = gate_up(a("ffn_Wsg").reshape(2, F, D), a("ffn_Wsu").reshape(2, F, D))
    arrays["sh_dn"] = a("ffn_Wsd").T.reshape(2, F, D)
    arrays["ex_gu"] = gate_up(a("ffn_Wg"), a("ffn_Wu"))
    arrays["ex_dn"] = a("ffn_Wd").transpose(0, 2, 1)
    arrays = {name: np.ascontiguousarray(v) for name, v in arrays.items()}

    nc = bacc.Bacc("TRN2", target_bir_lowering=False, num_devices=1)
    io = {name: nc.dram_tensor("in_" + name, v.shape, mybir.dt.from_np(v.dtype), kind="ExternalInput").ap()
          for name, v in arrays.items()}
    out = nc.dram_tensor("out", (B, T, D), F32, kind="ExternalOutput").ap()
    build(nc, io, out)
    r = run(nc, [{"in_" + name: v for name, v in arrays.items()}], core_ids=[0])
    return r.results[0]["out"]
```
